# Optimizing a Trainium2 kernel written in Bass

```python
import numpy as np
import jax
import jax.numpy as jnp

def _softmax(x, axis=-1):
    return jax.nn.softmax(x, axis=axis)

def _gelu(x):
    return jax.nn.gelu(x, approximate=True)

def _silu(x):
    return jax.nn.silu(x)

def _sigmoid(x):
    return jax.nn.sigmoid(x)

def _layernorm(x, axis=-1, eps=1e-05):
    m = jnp.mean(x, axis=axis, keepdims=True)
    v = jnp.var(x, axis=axis, keepdims=True)
    return (x - m) / jnp.sqrt(v + eps)

def _scatter_add(tgt, idx, src, axis=0):
    return tgt.at[idx].add(src)

def _segment_sum(src, seg, n):
    return jax.ops.segment_sum(src, seg, n)
kernel_name = 'mk_gps_d2_gnn_r64_a6e6fc'

def setup_inputs(seed: int=0):
    np.random.seed(seed)
    _w = jnp.asarray

    def _rec_inputs():
        import jax
        import jax.numpy as jnp
        _gk = jax.random.key(seed)
        x = -0.000125 + 0.9999 * jax.random.normal(jax.random.fold_in(_gk, 1), (1024, 512), jnp.float32)
        src = jax.random.randint(jax.random.fold_in(_gk, 2), (16384,), 0, 1024, jnp.int32)
        dst = jnp.minimum((1024 * jax.random.uniform(jax.random.fold_in(_gk, 3), (16384,)) ** 2.0).astype(jnp.int32), 65535)
        _o = jnp.argsort(dst, stable=True)
        src = src[_o]
        dst = dst[_o]
        edge_weight = jax.random.uniform(jax.random.fold_in(_gk, 12), (16384,), jnp.float32, 0.0, 0.999998)
        return (x, src, dst, edge_weight)
    x, src, dst, edge_weight = _rec_inputs()

    def _L0_gnn_setup():
        import jax, jax.numpy as jnp
        import numpy as np
        N_NODES = 1024
        N_EDGES = 8192
        FEAT_DIM = 512
        EMBED_DIM = 512
        key = jax.random.key(seed)
        k1, k2, k3, k4, k5 = jax.random.split(key, 5)
        x = jax.random.normal(k1, (N_NODES, FEAT_DIM), dtype=jnp.float32)
        limit = float(np.sqrt(6.0 / (EMBED_DIM + FEAT_DIM)))
        weight = jax.random.uniform(k2, (EMBED_DIM, FEAT_DIM), dtype=jnp.float32, minval=-limit, maxval=limit)
        row = jax.random.randint(k3, (N_EDGES,), 0, N_NODES, dtype=jnp.int64)
        col = jax.random.randint(k4, (N_EDGES,), 0, N_NODES, dtype=jnp.int64)
        vals = jax.random.uniform(k5, (N_EDGES,), dtype=jnp.float32)
        return {'x': x, 'weight': weight, 'row': row, 'col': col, 'vals': vals}
    _L0_gnn_all = _L0_gnn_setup()
    _L0_gnn_in = {k: v for k, v in _L0_gnn_all.items() if k in ('weight',)}
    del _L0_gnn_all

    def _L0_mix_setup():
        import jax, jax.numpy as jnp
        import numpy as np
        DEPTH, DIM, HEADS, DIM_HEAD, NBF, MULT = (2, 512, 8, 64, 256, 4)
        INNER = HEADS * DIM_HEAD

        def layernorm(x, g, b, eps=1e-05):
            mu = jnp.mean(x, axis=-1, keepdims=True)
            var = jnp.mean((x - mu) ** 2, axis=-1, keepdims=True)
            return (x - mu) * jax.lax.rsqrt(var + eps) * g + b

        def softmax_kernel(data, proj, is_query, eps=0.0001):
            d = data.shape[-1]
            normalizer = d ** (-0.25)
            ratio = proj.shape[0] ** (-0.5)
            data_dash = jnp.einsum('bhnd,md->bhnm', data * normalizer, proj)
            diag = jnp.sum(data ** 2, axis=-1, keepdims=True) * 0.5 * normalizer ** 2
            if is_query:
                m = jnp.max(data_dash, axis=-1, keepdims=True)
            else:
                m = jnp.max(data_dash, axis=(-2, -1), keepdims=True)
            m = jax.lax.stop_gradient(m)
            return ratio * (jnp.exp(data_dash - diag - m) + eps)
        key = jax.random.key(seed)
        ks = jax.random.split(key, 16)
        s = 0.02
        B, N = (4, 128)
        inp = {'x': jax.random.normal(ks[0], (B, N, DIM), jnp.float32), 'ln1_g': jnp.ones((DEPTH, DIM), jnp.float32), 'ln1_b': jnp.zeros((DEPTH, DIM), jnp.float32), 'ln2_g': jnp.ones((DEPTH, DIM), jnp.float32), 'ln2_b': jnp.zeros((DEPTH, DIM), jnp.float32), 'Wq': jax.random.normal(ks[1], (DEPTH, DIM, INNER), jnp.float32) * s, 'bq': jnp.zeros((DEPTH, INNER), jnp.float32), 'Wk': jax.random.normal(ks[2], (DEPTH, DIM, INNER), jnp.float32) * s, 'bk': jnp.zeros((DEPTH, INNER), jnp.float32), 'Wv': jax.random.normal(ks[3], (DEPTH, DIM, INNER), jnp.float32) * s, 'bv': jnp.zeros((DEPTH, INNER), jnp.float32), 'Wo': jax.random.normal(ks[4], (DEPTH, INNER, DIM), jnp.float32) * s, 'bo': jnp.zeros((DEPTH, DIM), jnp.float32), 'proj': jax.random.normal(ks[5], (DEPTH, NBF, DIM_HEAD), jnp.float32), 'W1': jax.random.normal(ks[6], (DEPTH, DIM, DIM * MULT), jnp.float32) * s, 'b1': jnp.zeros((DEPTH, DIM * MULT), jnp.float32), 'W2': jax.random.normal(ks[7], (DEPTH, DIM * MULT, DIM), jnp.float32) * s, 'b2': jnp.zeros((DEPTH, DIM), jnp.float32)}
        return inp
    _L0_mix_all = _L0_mix_setup()
    _L0_mix_in = {k: v for k, v in _L0_mix_all.items() if k in ('ln1_g', 'ln1_b', 'ln2_g', 'ln2_b', 'Wq', 'bq', 'Wk', 'bk', 'Wv', 'bv', 'Wo', 'bo', 'proj', 'W1', 'b1', 'W2', 'b2')}
    del _L0_mix_all

    def _L0_ffn_setup():
        import jax, jax.numpy as jnp
        import numpy as np
        ROUTER_JITTER = 0.01
        NEG_INF = -jnp.inf

        def _sparsemixer_eval(scores, num_experts):
            eids = jnp.arange(num_experts)
            max1 = jnp.max(scores, axis=-1, keepdims=True)
            sel1 = jnp.argmax(scores, axis=-1)
            factor1 = jnp.maximum(jnp.abs(scores), max1)
            mask1 = (max1 - scores) / factor1 > 2.0 * ROUTER_JITTER
            mg1 = jnp.where(mask1, NEG_INF, scores)
            p1 = jax.nn.softmax(mg1, axis=-1)
            mult1 = jnp.take_along_axis(p1, sel1[:, None], axis=-1)[:, 0]
            oh1 = sel1[:, None] == eids[None, :]
            masked_scores = jnp.where(oh1, NEG_INF, scores)
            max2 = jnp.max(masked_scores, axis=-1, keepdims=True)
            sel2 = jnp.argmax(masked_scores, axis=-1)
            factor2 = jnp.maximum(jnp.abs(scores), max2)
            mask2 = (max2 - scores) / factor2 > 2.0 * ROUTER_JITTER
            mg2 = jnp.where(mask2, NEG_INF, masked_scores)
            p2 = jax.nn.softmax(mg2, axis=-1)
            mult2 = jnp.take_along_axis(p2, sel2[:, None], axis=-1)[:, 0]
            weights = jnp.stack([mult1, mult2], axis=-1)
            experts = jnp.stack([sel1, sel2], axis=-1)
            return (weights, experts)
        B, S, H, F, E = (2, 32, 512, 1024, 8)
        key = jax.random.key(seed)
        ks = jax.random.split(key, 6)
        scale_h = 1.0 / np.sqrt(H)
        scale_f = 1.0 / np.sqrt(F)
        return {'x': jax.random.normal(ks[0], (B, S, H), dtype=jnp.float32), 'wg': jax.random.normal(ks[1], (H, E), dtype=jnp.float32) * scale_h, 'bg': jax.random.normal(ks[2], (E,), dtype=jnp.float32) * 0.01, 'w1': jax.random.normal(ks[3], (E, H, F), dtype=jnp.float32) * scale_h, 'w3': jax.random.normal(ks[4], (E, H, F), dtype=jnp.float32) * scale_h, 'w2': jax.random.normal(ks[5], (E, F, H), dtype=jnp.float32) * scale_f}
    _L0_ffn_all = _L0_ffn_setup()
    _L0_ffn_in = {k: v for k, v in _L0_ffn_all.items() if k in ('wg', 'bg', 'w1', 'w3', 'w2')}
    del _L0_ffn_all

    def _L1_gnn_setup():
        import jax, jax.numpy as jnp
        import numpy as np
        N, E, D_IN, D_H = (20000, 5000, 512, 512)
        ALPHA = 0.1
        LAMBDA = 1.0

        def _gcn2_layer(h, h0, src, dst, norm, w1, w2, b, layer):
            beta = float(np.log(LAMBDA / layer + 1.0))
            x = h * norm
            agg = jax.ops.segment_sum(x[src], dst, num_segments=h.shape[0])
            agg = agg * norm
            f = agg * (1.0 - ALPHA)
            f0 = h0 * ALPHA
            rst = (1.0 - beta) * f + beta * (f @ w1) + (1.0 - beta) * f0 + beta * (f0 @ w2) + b
            return jax.nn.relu(rst)
        key = jax.random.key(seed)
        ks = jax.random.split(key, 12)
        feat = jax.random.normal(ks[0], (N, D_IN), dtype=jnp.float32)
        src = jax.random.randint(ks[1], (E,), 0, N, dtype=jnp.int32)
        dst = jax.random.randint(ks[2], (E,), 0, N, dtype=jnp.int32)
        s = 0.05
        fc_w = jax.random.normal(ks[3], (D_H, D_IN), dtype=jnp.float32) * s
        fc_b = jax.random.normal(ks[4], (D_H,), dtype=jnp.float32) * s
        w1_1 = jax.random.normal(ks[5], (D_H, D_H), dtype=jnp.float32) * s
        w2_1 = jax.random.normal(ks[6], (D_H, D_H), dtype=jnp.float32) * s
        b_1 = jax.random.normal(ks[7], (D_H,), dtype=jnp.float32) * s
        w1_2 = jax.random.normal(ks[8], (D_H, D_H), dtype=jnp.float32) * s
        w2_2 = jax.random.normal(ks[9], (D_H, D_H), dtype=jnp.float32) * s
        b_2 = jax.random.normal(ks[10], (D_H,), dtype=jnp.float32) * s
        return {'feat': feat, 'src': src, 'dst': dst, 'fc_w': fc_w, 'fc_b': fc_b, 'w1_1': w1_1, 'w2_1': w2_1, 'b_1': b_1, 'w1_2': w1_2, 'w2_2': w2_2, 'b_2': b_2}
    _L1_gnn_all = _L1_gnn_setup()
    _L1_gnn_in = {k: v for k, v in _L1_gnn_all.items() if k in ('fc_w', 'fc_b', 'w1_1', 'w2_1', 'b_1', 'w1_2', 'w2_2', 'b_2')}
    del _L1_gnn_all

    def _L1_mix_setup():
        import jax, jax.numpy as jnp
        import numpy as np
        import math
        D_MODEL = 512
        key = jax.random.key(seed)
        k1, k2, k3 = jax.random.split(key, 3)
        X = jax.random.normal(k1, (4, 128, D_MODEL), dtype=jnp.float32)
        s = 1.0 / math.sqrt(D_MODEL)
        W_v = jax.random.uniform(k2, (D_MODEL, D_MODEL), dtype=jnp.float32, minval=-s, maxval=s)
        W_theta = jax.random.uniform(k3, (D_MODEL, D_MODEL), dtype=jnp.float32, minval=-s, maxval=s)
        return {'X': X, 'W_v': W_v, 'W_theta': W_theta}
    _L1_mix_all = _L1_mix_setup()
    _L1_mix_in = {k: v for k, v in _L1_mix_all.items() if k in ('W_v', 'W_theta')}
    del _L1_mix_all

    def _L1_ffn_setup():
        import jax, jax.numpy as jnp
        import numpy as np
        MARK_AX, OP_ADD, OP_SUB = (0, 1, 2)
        ALU_LO, ALU_HI = (16, 32)
        AX_CARRY_LO, AX_CARRY_HI = (48, 64)
        OPCODE_BASE = 80
        OUTPUT_LO, OUTPUT_HI, CARRY = (128, 144, 160)
        NIB_A, NIB_B, OP_START = (0, 1, 10)
        RESULT, CARRY_OUT = (100, 101)
        GE_POS, GE_DIM = (8, 160)
        OPC_ADD, OPC_SUB = (25, 26)
        B, S, D = (8, 64, 512)

        def _decode_nibble(x, base):
            return jnp.argmax(x[..., base:base + 16] > 0.5, axis=-1).astype(x.dtype)

        def _pipeline(h, W, b):
            for i in range(3):
                h = jnp.einsum('bspd,od->bspo', h, W[i]) + b[i]
                if i < 2:
                    h = jax.nn.relu(h)
            return h
        key = jax.random.key(seed)
        kx, k1, k2, k3, k4 = jax.random.split(key, 5)
        x_bd = jax.random.uniform(kx, (B, S, D), dtype=jnp.float32)
        Wa = jax.random.normal(k1, (3, GE_DIM, GE_DIM), dtype=jnp.float32) * 0.05
        ba = jax.random.normal(k2, (3, GE_DIM), dtype=jnp.float32) * 0.05
        Ws = jax.random.normal(k3, (3, GE_DIM, GE_DIM), dtype=jnp.float32) * 0.05
        bs = jax.random.normal(k4, (3, GE_DIM), dtype=jnp.float32) * 0.05
        return {'x_bd': x_bd, 'Wa': Wa, 'ba': ba, 'Ws': Ws, 'bs': bs}
    _L1_ffn_all = _L1_ffn_setup()
    _L1_ffn_in = {k: v for k, v in _L1_ffn_all.items() if k in ('Wa', 'ba', 'Ws', 'bs')}
    del _L1_ffn_all
    return {'x': x, 'src': src, 'dst': dst, 'edge_weight': edge_weight, 'L0_gnn_weight': _L0_gnn_in['weight'], 'L0_mix_ln1_g': _L0_mix_in['ln1_g'], 'L0_mix_ln1_b': _L0_mix_in['ln1_b'], 'L0_mix_ln2_g': _L0_mix_in['ln2_g'], 'L0_mix_ln2_b': _L0_mix_in['ln2_b'], 'L0_mix_Wq': _L0_mix_in['Wq'], 'L0_mix_bq': _L0_mix_in['bq'], 'L0_mix_Wk': _L0_mix_in['Wk'], 'L0_mix_bk': _L0_mix_in['bk'], 'L0_mix_Wv': _L0_mix_in['Wv'], 'L0_mix_bv': _L0_mix_in['bv'], 'L0_mix_Wo': _L0_mix_in['Wo'], 'L0_mix_bo': _L0_mix_in['bo'], 'L0_mix_proj': _L0_mix_in['proj'], 'L0_mix_W1': _L0_mix_in['W1'], 'L0_mix_b1': _L0_mix_in['b1'], 'L0_mix_W2': _L0_mix_in['W2'], 'L0_mix_b2': _L0_mix_in['b2'], 'L0_ffn_wg': _L0_ffn_in['wg'], 'L0_ffn_bg': _L0_ffn_in['bg'], 'L0_ffn_w1': _L0_ffn_in['w1'], 'L0_ffn_w3': _L0_ffn_in['w3'], 'L0_ffn_w2': _L0_ffn_in['w2'], 'L1_gnn_fc_w': _L1_gnn_in['fc_w'], 'L1_gnn_fc_b': _L1_gnn_in['fc_b'], 'L1_gnn_w1_1': _L1_gnn_in['w1_1'], 'L1_gnn_w2_1': _L1_gnn_in['w2_1'], 'L1_gnn_b_1': _L1_gnn_in['b_1'], 'L1_gnn_w1_2': _L1_gnn_in['w1_2'], 'L1_gnn_w2_2': _L1_gnn_in['w2_2'], 'L1_gnn_b_2': _L1_gnn_in['b_2'], 'L1_mix_W_v': _L1_mix_in['W_v'], 'L1_mix_W_theta': _L1_mix_in['W_theta'], 'L1_ffn_Wa': _L1_ffn_in['Wa'], 'L1_ffn_ba': _L1_ffn_in['ba'], 'L1_ffn_Ws': _L1_ffn_in['Ws'], 'L1_ffn_bs': _L1_ffn_in['bs']}

def reference(x, src, dst, edge_weight, L0_gnn_weight, L0_mix_ln1_g, L0_mix_ln1_b, L0_mix_ln2_g, L0_mix_ln2_b, L0_mix_Wq, L0_mix_bq, L0_mix_Wk, L0_mix_bk, L0_mix_Wv, L0_mix_bv, L0_mix_Wo, L0_mix_bo, L0_mix_proj, L0_mix_W1, L0_mix_b1, L0_mix_W2, L0_mix_b2, L0_ffn_wg, L0_ffn_bg, L0_ffn_w1, L0_ffn_w3, L0_ffn_w2, L1_gnn_fc_w, L1_gnn_fc_b, L1_gnn_w1_1, L1_gnn_w2_1, L1_gnn_b_1, L1_gnn_w1_2, L1_gnn_w2_2, L1_gnn_b_2, L1_mix_W_v, L1_mix_W_theta, L1_ffn_Wa, L1_ffn_ba, L1_ffn_Ws, L1_ffn_bs):
    import jax
    import jax.numpy as jnp

    def _L0_gnn_ref(x, weight, row, col, vals):
        import jax, jax.numpy as jnp
        import numpy as np
        N_NODES = 1024
        N_EDGES = 8192
        FEAT_DIM = 512
        EMBED_DIM = 512
        h = jnp.einsum('nf,ef->ne', x, weight)
        msgs = vals[:, None] * h[col]
        out = jax.ops.segment_sum(msgs, row, num_segments=N_NODES)
        return out

    def _L0_mix_ref(x, ln1_g, ln1_b, ln2_g, ln2_b, Wq, bq, Wk, bk, Wv, bv, Wo, bo, proj, W1, b1, W2, b2):
        import jax, jax.numpy as jnp
        import numpy as np
        DEPTH, DIM, HEADS, DIM_HEAD, NBF, MULT = (2, 512, 8, 64, 256, 4)
        INNER = HEADS * DIM_HEAD

        def layernorm(x, g, b, eps=1e-05):
            mu = jnp.mean(x, axis=-1, keepdims=True)
            var = jnp.mean((x - mu) ** 2, axis=-1, keepdims=True)
            return (x - mu) * jax.lax.rsqrt(var + eps) * g + b

        def softmax_kernel(data, proj, is_query, eps=0.0001):
            d = data.shape[-1]
            normalizer = d ** (-0.25)
            ratio = proj.shape[0] ** (-0.5)
            data_dash = jnp.einsum('bhnd,md->bhnm', data * normalizer, proj)
            diag = jnp.sum(data ** 2, axis=-1, keepdims=True) * 0.5 * normalizer ** 2
            if is_query:
                m = jnp.max(data_dash, axis=-1, keepdims=True)
            else:
                m = jnp.max(data_dash, axis=(-2, -1), keepdims=True)
            m = jax.lax.stop_gradient(m)
            return ratio * (jnp.exp(data_dash - diag - m) + eps)
        B, N, D = x.shape
        for i in range(DEPTH):
            y = layernorm(x, ln1_g[i], ln1_b[i])
            q = (y @ Wq[i] + bq[i]).reshape(B, N, HEADS, DIM_HEAD).transpose(0, 2, 1, 3)
            k = (y @ Wk[i] + bk[i]).reshape(B, N, HEADS, DIM_HEAD).transpose(0, 2, 1, 3)
            v = (y @ Wv[i] + bv[i]).reshape(B, N, HEADS, DIM_HEAD).transpose(0, 2, 1, 3)
            qp = softmax_kernel(q, proj[i], True)
            kp = softmax_kernel(k, proj[i], False)
            k_sum = kp.sum(axis=2)
            d_inv = 1.0 / jnp.einsum('bhnm,bhm->bhn', qp, k_sum)
            ctx = jnp.einsum('bhnm,bhnd->bhmd', kp, v)
            o = jnp.einsum('bhmd,bhnm,bhn->bhnd', ctx, qp, d_inv)
            o = o.transpose(0, 2, 1, 3).reshape(B, N, INNER)
            x = x + o @ Wo[i] + bo[i]
            y = layernorm(x, ln2_g[i], ln2_b[i])
            h = jax.nn.gelu(y @ W1[i] + b1[i], approximate=False)
            x = x + h @ W2[i] + b2[i]
        return x

    def _L0_ffn_ref(x, wg, bg, w1, w3, w2):
        import jax, jax.numpy as jnp
        import numpy as np
        ROUTER_JITTER = 0.01
        NEG_INF = -jnp.inf

        def _sparsemixer_eval(scores, num_experts):
            eids = jnp.arange(num_experts)
            max1 = jnp.max(scores, axis=-1, keepdims=True)
            sel1 = jnp.argmax(scores, axis=-1)
            factor1 = jnp.maximum(jnp.abs(scores), max1)
            mask1 = (max1 - scores) / factor1 > 2.0 * ROUTER_JITTER
            mg1 = jnp.where(mask1, NEG_INF, scores)
            p1 = jax.nn.softmax(mg1, axis=-1)
            mult1 = jnp.take_along_axis(p1, sel1[:, None], axis=-1)[:, 0]
            oh1 = sel1[:, None] == eids[None, :]
            masked_scores = jnp.where(oh1, NEG_INF, scores)
            max2 = jnp.max(masked_scores, axis=-1, keepdims=True)
            sel2 = jnp.argmax(masked_scores, axis=-1)
            factor2 = jnp.maximum(jnp.abs(scores), max2)
            mask2 = (max2 - scores) / factor2 > 2.0 * ROUTER_JITTER
            mg2 = jnp.where(mask2, NEG_INF, masked_scores)
            p2 = jax.nn.softmax(mg2, axis=-1)
            mult2 = jnp.take_along_axis(p2, sel2[:, None], axis=-1)[:, 0]
            weights = jnp.stack([mult1, mult2], axis=-1)
            experts = jnp.stack([sel1, sel2], axis=-1)
            return (weights, experts)
        B, S, H = x.shape
        E = w1.shape[0]
        xt = x.reshape(-1, H)
        scores = jax.nn.softmax(xt @ wg + bg, axis=-1)
        routing_weights, selected_experts = _sparsemixer_eval(scores, E)
        eids = jnp.arange(E)
        comb = jnp.sum(routing_weights[:, :, None] * (selected_experts[:, :, None] == eids[None, None, :]).astype(xt.dtype), axis=1)
        out = jnp.zeros_like(xt)
        for e in range(E):
            h = jax.nn.gelu(xt @ w1[e], approximate=False) * (xt @ w3[e])
            out = out + comb[:, e:e + 1] * (h @ w2[e])
        return out.reshape(B, S, H)

    def _L1_gnn_ref(feat, src, dst, fc_w, fc_b, w1_1, w2_1, b_1, w1_2, w2_2, b_2):
        import jax, jax.numpy as jnp
        import numpy as np
        N, E, D_IN, D_H = (20000, 5000, 512, 512)
        ALPHA = 0.1
        LAMBDA = 1.0

        def _gcn2_layer(h, h0, src, dst, norm, w1, w2, b, layer):
            beta = float(np.log(LAMBDA / layer + 1.0))
            x = h * norm
            agg = jax.ops.segment_sum(x[src], dst, num_segments=h.shape[0])
            agg = agg * norm
            f = agg * (1.0 - ALPHA)
            f0 = h0 * ALPHA
            rst = (1.0 - beta) * f + beta * (f @ w1) + (1.0 - beta) * f0 + beta * (f0 @ w2) + b
            return jax.nn.relu(rst)
        n = feat.shape[0]
        h = feat @ fc_w.T + fc_b
        deg = jax.ops.segment_sum(jnp.ones_like(dst, dtype=h.dtype), dst, num_segments=n)
        norm = jnp.clip(deg, 1.0, None) ** (-0.5)
        norm = norm[:, None]
        res = _gcn2_layer(h, h, src, dst, norm, w1_1, w2_1, b_1, layer=1)
        out = _gcn2_layer(res, h, src, dst, norm, w1_2, w2_2, b_2, layer=2)
        return out

    def _L1_mix_ref(X, W_v, W_theta):
        import jax, jax.numpy as jnp
        import numpy as np
        import math
        D_MODEL = 512
        n = X.shape[1]
        d = X.shape[2]
        XW_v = X @ W_v.T
        theta_X = X @ W_theta.T
        first_term = jnp.mean(XW_v, axis=1, keepdims=True)
        kv = jnp.einsum('bnd,bne->bde', theta_X, XW_v)
        second_term = X @ kv / (n * math.sqrt(d))
        return first_term + second_term

    def _L1_ffn_ref(x_bd, Wa, ba, Ws, bs):
        import jax, jax.numpy as jnp
        import numpy as np
        MARK_AX, OP_ADD, OP_SUB = (0, 1, 2)
        ALU_LO, ALU_HI = (16, 32)
        AX_CARRY_LO, AX_CARRY_HI = (48, 64)
        OPCODE_BASE = 80
        OUTPUT_LO, OUTPUT_HI, CARRY = (128, 144, 160)
        NIB_A, NIB_B, OP_START = (0, 1, 10)
        RESULT, CARRY_OUT = (100, 101)
        GE_POS, GE_DIM = (8, 160)
        OPC_ADD, OPC_SUB = (25, 26)
        B, S, D = (8, 64, 512)

        def _decode_nibble(x, base):
            return jnp.argmax(x[..., base:base + 16] > 0.5, axis=-1).astype(x.dtype)

        def _pipeline(h, W, b):
            for i in range(3):
                h = jnp.einsum('bspd,od->bspo', h, W[i]) + b[i]
                if i < 2:
                    h = jax.nn.relu(h)
            return h
        x = x_bd
        Bsz, seq, _ = x.shape
        x_ge = jnp.zeros((Bsz, seq, GE_POS, GE_DIM), dtype=x.dtype)
        x_ge = x_ge.at[..., 0, NIB_A].set(_decode_nibble(x, ALU_LO))
        x_ge = x_ge.at[..., 1, NIB_A].set(_decode_nibble(x, ALU_HI))
        x_ge = x_ge.at[..., 0, NIB_B].set(_decode_nibble(x, AX_CARRY_LO))
        x_ge = x_ge.at[..., 1, NIB_B].set(_decode_nibble(x, AX_CARRY_HI))
        x_ge = x_ge.at[..., :, OP_START + OPC_ADD].set(x[..., OPCODE_BASE + OPC_ADD][..., None])
        x_ge = x_ge.at[..., :, OP_START + OPC_SUB].set(x[..., OPCODE_BASE + OPC_SUB][..., None])
        mark = x[..., MARK_AX] > 0.5
        m_add = mark & (x[..., OP_ADD] > 0.5)
        m_sub = mark & ~(x[..., OP_ADD] > 0.5) & (x[..., OP_SUB] > 0.5)
        active = (m_add | m_sub).astype(x.dtype)
        y_add = _pipeline(x_ge, Wa, ba)
        y_sub = _pipeline(x_ge, Ws, bs)
        y = jnp.where(m_add[..., None, None], y_add, jnp.where(m_sub[..., None, None], y_sub, x_ge))
        res_lo = jnp.clip(jnp.round(y[..., 0, RESULT]), 0, 15).astype(jnp.int32)
        res_hi = jnp.clip(jnp.round(y[..., 1, RESULT]), 0, 15).astype(jnp.int32)
        oh_lo = jax.nn.one_hot(res_lo, 16, dtype=x.dtype) * active[..., None]
        oh_hi = jax.nn.one_hot(res_hi, 16, dtype=x.dtype) * active[..., None]
        carry = (jnp.round(y[..., 1, CARRY_OUT]) > 0.5).astype(x.dtype) * active
        out = x
        out = out.at[..., OUTPUT_LO:OUTPUT_LO + 16].add(2.0 * oh_lo)
        out = out.at[..., OUTPUT_HI:OUTPUT_HI + 16].add(2.0 * oh_hi)
        out = out.at[..., CARRY].add(carry)
        return out
    xn = _layernorm(x, axis=-1)
    x = x + _L0_gnn_ref(xn, L0_gnn_weight, src, dst, edge_weight) + _L0_mix_ref(xn[None], L0_mix_ln1_g, L0_mix_ln1_b, L0_mix_ln2_g, L0_mix_ln2_b, L0_mix_Wq, L0_mix_bq, L0_mix_Wk, L0_mix_bk, L0_mix_Wv, L0_mix_bv, L0_mix_Wo, L0_mix_bo, L0_mix_proj, L0_mix_W1, L0_mix_b1, L0_mix_W2, L0_mix_b2)[0]
    x = x + _L0_ffn_ref(_layernorm(x, axis=-1)[None], L0_ffn_wg, L0_ffn_bg, L0_ffn_w1, L0_ffn_w3, L0_ffn_w2)[0]
    xn = _layernorm(x, axis=-1)
    x = x + _L1_gnn_ref(xn, src, dst, L1_gnn_fc_w, L1_gnn_fc_b, L1_gnn_w1_1, L1_gnn_w2_1, L1_gnn_b_1, L1_gnn_w1_2, L1_gnn_w2_2, L1_gnn_b_2) + _L1_mix_ref(xn[None], L1_mix_W_v, L1_mix_W_theta)[0]
    x = x + _L1_ffn_ref(_layernorm(x, axis=-1)[None], L1_ffn_Wa, L1_ffn_ba, L1_ffn_Ws, L1_ffn_bs)[0]
    return x

_drawn_inputs = setup_inputs


def setup_inputs(seed=0):
    import zlib

    import numpy as np

    out = dict(_drawn_inputs(seed))
    spreads = {'L0_mix_ln1_g': (1.0, 0.6),
     'L0_mix_ln1_b': (0.0, 0.293),
     'L0_mix_ln2_g': (1.0, 0.2),
     'L0_mix_ln2_b': (0.0, 0.281),
     'L0_mix_bq': (0.0, 0.8),
     'L0_mix_bk': (0.0, 0.8),
     'L0_mix_bv': (0.0, 0.1),
     'L0_mix_bo': (0.0, 0.1),
     'L0_mix_b1': (0.0, 0.1),
     'L0_mix_b2': (0.0, 0.1)}
    factors = {'L0_mix_Wq': 6.965,
     'L0_mix_Wk': 7.982,
     'L0_mix_proj': 7.01,
     'L0_ffn_bg': 2.677,
     'L1_gnn_fc_b': 8.0,
     'L1_gnn_w1_1': 4.071,
     'L1_gnn_w2_1': 8.0,
     'L1_gnn_b_1': 8.0,
     'L1_gnn_w1_2': 3.301,
     'L1_gnn_w2_2': 5.02,
     'L1_gnn_b_2': 4.906,
     'L1_mix_W_theta': 7.503}
    for name, (base, spread) in spreads.items():
        noise = np.random.default_rng([zlib.crc32(name.encode()), seed]).standard_normal(out[name].shape)
        drawn = base * np.exp(spread * noise) if base else spread * noise
        out[name] = jnp.asarray(drawn.astype(out[name].dtype))
    for name, factor in factors.items():
        out[name] = (out[name] * factor).astype(out[name].dtype)
    return out
```

```python
from contextlib import ExitStack
import math

import numpy as np
import concourse.bass as bass
from concourse import mybir

F32 = mybir.dt.float32
F32R = mybir.dt.float32r
I32 = mybir.dt.int32
U32 = mybir.dt.uint32
ALU = mybir.AluOpType
ACT = mybir.ActivationFunctionType
AX_X = mybir.AxisListType.X

P = 128
N = 1024
D = 512
NT = N // P
NK = D // P
HALF = 512
NE = 16384
EC = NE // P
EB = 4
TABLE = N * N
HEADS, DH, NBF = 8, 64, 256
VW = DH + 1
MLP = 4
EXPERTS, EF = 8, 1024
FB = EF // D
DEPTH = 2
LN_EPS = 1e-5
KERNEL_EPS = 1e-4
NORMALIZER = DH ** -0.25
JITTER = 2.0 * 0.01
GE = 160
GE_LO = GE - P
RESULT, OUT_LO, CARRY = 100, 128, 160
ROUNDER = 1.5 * 2.0 ** 23
BLK = 2048
SLOTS = 3
BANKS = 8
JOBS_PER_EXPERT = FB * 24


def job_plan():
    stages = [("xn_T", 8, "AD"), ("gnn_w_T", 4, "AD"), ("hg", 8, "A"), ("edge_T", 1, "D")]
    for l in range(DEPTH):
        stages += [(f"y_T{l}", 8, "AD"), (f"proj{l}", 1, "A"), (f"q{l}", 8, "A"), (f"dq{l}", 1, "A"), (f"k{l}", 8, "A"),
                   (f"dk{l}", 1, "A"), (f"v{l}", 8, "D"), (f"vsum{l}", 1, "A")]
        for hp in range(HEADS // 2):
            s = f"{l}.{hp}"
            stages += [("kd" + s, 8, "AD"), ("qd" + s, 8, "D"), ("eT_a" + s, 4, "D"), ("ctx" + s, 1, "D"), ("csum" + s, 1, "A"),
                       ("o_a" + s, 4, "D"), ("eT_b" + s, 4, "D"), ("o_b" + s, 4, "D")]
        stages += [(f"o_T{l}", 8, "AD"), (f"wo{l}", 8, "D"), (f"y2_T{l}", 8, "AD")]
        for fb in range(MLP):
            stages += [(f"up{l}.{fb}", 8, "A"), (f"down{l}.{fb}", 8, "D")]
    stages += [("gnn", 8, "D"), ("xt_T", 8, "AD"), ("gate", 1, "D")]
    for e in range(EXPERTS):
        for fb in range(FB):
            for j in range(8):
                stages += [(f"e{e}.{fb}.gate{j}", 1, "A"), (f"e{e}.{fb}.up{j}", 1, "D")]
            stages.append((f"e{e}.{fb}.down", 8, "D"))
    stages += [("x3_T", 8, "AD"), ("deg", 1, "D"), ("wv_T", 4, "AD"), ("xwv", 8, "A"), ("wth_T", 4, "AD"), ("theta", 8, "A"),
               ("kv", 4, "AD"), ("mean", 1, "A"), ("xkv", 8, "D"), ("fc_T", 4, "AD"), ("h", 8, "D"), ("h_T", 8, "AD")]
    for g in range(2):
        stages += [(f"agg{g}", 8, "D"), (f"f_T{g}", 8, "AD"), (f"rst{g}", 8, "D")]
    stages += [("u_T", 4, "D"), ("w1_T", 2, "D")]
    for i in range(8):
        stages += [(f"alu{i}", 4, "A"), (f"alu_out{i}", 1, "D")]
    first, who, acts, dones = {}, [], [], []
    for name, count, engines in stages:
        first[name] = len(who)
        for _ in range(count):
            who.append(engines)
            acts.append((acts[-1] if acts else 0) + ("A" in engines))
            dones.append((dones[-1] if dones else 0) + ("D" in engines))
    first["experts"], first["alu"] = first["e0.0.gate0"], first["alu0"]
    return first, who, acts, dones


JOB, WHO, ACTS, DONES = job_plan()
ACTS_PER_EXPERT, DONES_PER_EXPERT = 8 * FB, 16 * FB


class Block:

    def __init__(self, name, kind, source, last_job):
        self.name, self.kind, self.source, self.last_job = name, kind, source, last_job


def gps_network(nc, a, out):
    x_in = a["x"]

    def square(w, col=0):
        return w[:, col:col + D].rearrange("(k p) n -> p k n", p=P)

    def rows(w, row):
        return w[row:row + D, :].rearrange("(k p) n -> p k n", p=P)

    hg_dram = nc.dram_tensor("hg_dram", (N, D), F32, kind="Internal").ap()
    key_dram = nc.dram_tensor("key_dram", (NE,), F32, kind="Internal").ap()
    table_w = nc.dram_tensor("table_w", (TABLE + P, 1), F32, kind="Internal").ap()
    table_c = nc.dram_tensor("table_c", (TABLE + P, 1), F32, kind="Internal").ap()

    def table_block(table, q):
        cells = table[0:TABLE, :].rearrange("(r p c) o -> p r (c o)", p=P, c=N)
        return cells[:, :, q * 256:(q + 1) * 256]

    blocks = [Block("gnn_w", "transpose", square(a["L0_gnn_weight"]), JOB["gnn_w_T"] + 3)]
    for l in range(DEPTH):
        blocks += [Block(f"wq{l}", "slot", square(a["L0_mix_Wq"][l]), JOB[f"q{l}"] + 7),
                   Block(f"wk{l}", "slot", square(a["L0_mix_Wk"][l]), JOB[f"k{l}"] + 7),
                   Block(f"wv{l}", "slot", square(a["L0_mix_Wv"][l]), JOB[f"v{l}"] + 7),
                   Block(f"wo{l}", "slot", square(a["L0_mix_Wo"][l]), JOB[f"wo{l}"] + 7)]
        for fb in range(MLP):
            blocks += [Block(f"up{l}.{fb}", "slot", square(a["L0_mix_W1"][l], fb * D), JOB[f"up{l}.{fb}"] + 7),
                       Block(f"down{l}.{fb}", "slot", rows(a["L0_mix_W2"][l], fb * D), JOB[f"down{l}.{fb}"] + 7)]
    for h in range(2):
        blocks.append(Block(f"hg{h}", "operand", rows(hg_dram, h * D), None))
    for h in range(2):
        blocks.append(Block(f"x{h}", "added", rows(x_in, h * D), None))
    for q in range(4):
        blocks.append(Block(f"adj{q}", "slot", table_block(table_w, q), JOB["gnn"] + 2 * q + 1))
    for e in range(EXPERTS):
        for fb in range(FB):
            j = JOB["experts"] + JOBS_PER_EXPERT * e + 24 * fb
            blocks += [Block(f"e{e}.w1.{fb}", "slot", None, j + 15), Block(f"e{e}.w3.{fb}", "slot", None, j + 15),
                       Block(f"e{e}.w2.{fb}", "slot", None, j + 23)]
    blocks += [Block(f"deg{q}", "counted", table_block(table_c, q), JOB["deg"]) for q in range(4)]
    blocks += [Block("l1_wv", "transpose", square(a["L1_mix_W_v"]), JOB["wv_T"] + 3),
               Block("l1_wth", "transpose", square(a["L1_mix_W_theta"]), JOB["wth_T"] + 3),
               Block("l1_fc", "transpose", square(a["L1_gnn_fc_w"]), JOB["fc_T"] + 3)]
    for g in range(2):
        blocks += [Block(f"cnt{g}.{q}", "slot", table_block(table_c, q), JOB[f"agg{g}"] + 2 * q + 1) for q in range(4)]
        blocks += [Block(f"gw1.{g}", "slot", square(a[f"L1_gnn_w1_{g + 1}"]), JOB[f"rst{g}"] + 7),
                   Block(f"gw2.{g}", "slot", square(a[f"L1_gnn_w2_{g + 1}"]), JOB[f"rst{g}"] + 7)]
    slot_order = ["gnn_w"]
    for l in range(DEPTH):
        slot_order += [f"wq{l}", f"wk{l}", f"wv{l}", f"wo{l}"]
        for fb in range(MLP):
            slot_order += [f"up{l}.{fb}", f"down{l}.{fb}"]
    slot_order += [f"adj{q}" for q in range(4)]
    for e in range(EXPERTS):
        for fb in range(FB):
            slot_order += [f"e{e}.w1.{fb}", f"e{e}.w3.{fb}", f"e{e}.w2.{fb}"]
    slot_order += ["l1_wv", "l1_wth", "kv", "l1_fc"]
    for g in range(2):
        slot_order += [f"cnt{g}.{q}" for q in range(4)] + [f"gw1.{g}", f"gw2.{g}"]
    slot_of = {name: i for i, name in enumerate(slot_order)}
    slot_last_job = {b.name: b.last_job for b in blocks}
    slot_last_job["kv"] = JOB["xkv"] + 7
    slot_last_job["gnn_w"] = JOB["hg"] + 7
    slot_last_job["l1_wv"] = JOB["xwv"] + 7
    slot_last_job["l1_wth"] = JOB["theta"] + 7
    slot_last_job["l1_fc"] = JOB["h"] + 7
    raw_no, split_no, split_count = {}, {}, 0
    for i, b in enumerate(blocks):
        raw_no[b.name] = i
        if b.kind in ("slot", "operand"):
            split_no[b.name] = split_count
            split_count += 1

    with ExitStack() as ctx:
        ctx.enter_context(nc.allow_non_contiguous_dma(reason="short parameter vectors laid out as columns"))

        def sem(name):
            return ctx.enter_context(nc.semaphore(name))

        top = [(nc.sbuf_base + 63) // 64 * 64]

        def region(nbytes):
            at = top[0]
            top[0] += (nbytes + 63) // 64 * 64
            assert top[0] <= nc.sbuf_usable_end, (top[0], nc.sbuf_usable_end)
            return at

        def place(name, shape, dtype=F32, at=None):
            size = 4
            for s in shape[1:]:
                size *= s
            return nc.alloc_sbuf_tensor_at(name, shape, dtype, offset=region(size) if at is None else at)

        X = place("X", [P, NT, D])
        at_a = region(2 * 4 * 4096)
        op_a = place("op_a", [P, 2, 4096], F32R, at_a)
        kd = place("kd", [P, 2, NT, NBF], F32, at_a)
        o_tok = place("o_tok", [P, NT, D], F32, at_a + 4 * 4096)
        at_b = region(2 * 4 * 4096)
        op_b = place("op_b", [P, 2, 4096], F32R, at_b)
        q_T = place("q_T", [P, NK, N], F32, at_b)
        k_T = place("k_T", [P, NK, N], F32, at_b + 4 * 4096)
        xwv = place("xwv", [P, NT, D], F32, at_b)
        theta = place("theta", [P, NT, D], F32, at_b + 4 * 4096)
        h1 = place("h1", [P, 4, HALF], F32, at_a)
        h2 = place("h2", [P, 4, HALF], F32, at_a + 4 * 4 * HALF)
        u_T = place("u_T", [4, 2, N], F32, at_b)
        G = place("G", [P, NT, D])
        W = place("W", [P, SLOTS, 2, BLK], F32R)
        raw = place("raw", [P, 2, BLK])
        at_v = region(4 * NT * HEADS * VW)
        V = place("V", [P, NT, HEADS, VW], F32, at_v)
        zero = place("zero", [P, 4096], F32, at_v)
        key_row = place("key_row", [P, EB, P], F32, at_v)
        w_row = place("w_row", [P, EB, P], F32, at_v + 2048)
        same = place("same", [P, EB, P], F32, at_v + 4096)
        picked = place("picked", [P, EB, P], F32, at_v + 6144)
        edge_int = place("edge_int", [P, 2, P], I32, at_v + 8192)
        edge_f = place("edge_f", [P, 5, P], F32, at_v + 10240)
        at_e = region(4 * 4 * 4 * P)
        E_T = place("E_T", [P, 4, 4, P], F32, at_e)
        tmp = place("tmp", [P, 2, D], F32, at_e)
        keycols = place("keycols", [P, 3, P])
        edge_ix = place("edge_ix", [P, 2, P], I32)
        edge_add = place("edge_add", [P, 2, P])
        batch = place("batch", [P, 4, EB])
        ident = place("ident", [P, P])
        lower = place("lower", [P, P])
        ones = place("ones", [P, P])
        eps_ones = place("eps_ones", [P, P])
        head_sel = place("head_sel", [P, 2])
        proj_nat = place("proj_nat", [P, 2, 2, DH])
        proj = place("proj", [P, 2, NBF])
        rowv = place("rowv", [P, 3, D])
        colv = place("colv", [P, DEPTH, 40])
        stats = place("stats", [P, 4, 6])
        mv = place("mv", [P, NT, 2])
        sd = place("sd", [P, NT])
        rstd = place("rstd", [P, NT])
        lneps = place("lneps", [P, 1])
        trash = place("trash", [P, 1])
        dexp = place("dexp", [P, 2, NT, HEADS])
        vsum = place("vsum", [P, HEADS, VW])
        kmax = place("kmax", [P, 2, NT])
        kmaxp = place("kmaxp", [P, 2, 2])
        nkmax = place("nkmax", [P, 2])
        nqmax = place("nqmax", [P, NT, 2])
        ctx_sb = place("ctx_sb", [P, 4, VW])
        csum = place("csum", [P, 2, VW])
        num = place("num", [P, 2, 2, VW])
        rden = place("rden", [P, 2, 2])
        wg_raw = place("wg_raw", [P, NK, EXPERTS])
        wg = place("wg", [P, 2, NK, EXPERTS], F32R)
        bg = place("bg", [P, EXPERTS])
        eidx = place("eidx", [P, EXPERTS])
        comb = place("comb", [P, NT, EXPERTS])
        g8 = place("g8", [P, 6, NT, EXPERTS], F32, at_v)
        g1 = place("g1", [P, 8, NT], F32, at_v + 4 * 6 * 64)
        combe = place("combe", [P, NT])
        norm = place("norm", [P, NT])
        mean_row = place("mean_row", [P, D], F32, at_v)
        w0_T = place("w0_T", [4, 2, GE], F32, at_v + 2048)
        wn_a = place("wn_a", [P, 2, GE], F32, at_v + 4096)
        wn_b = place("wn_b", [GE_LO, 2, GE], F32, at_v + 5632)
        w1_T = place("w1_T", [P, 2, 2, GE], F32, at_v + 7168)
        w2_T = place("w2_T", [P, 2, 2, 2], F32, at_v + 9792)
        b_hid = place("b_hid", [P, 2, 2, 2], F32, at_v + 9856)
        b_out = place("b_out", [P, 2, 2], F32, at_v + 9920)
        yo = place("yo", [P, 2, 2, NT, 2], F32, at_v + 9984)
        nib = place("nib", [P, NT, 4, 16], F32, at_v + 10496)
        nibv = place("nibv", [P, 3, NT, 4], F32, at_v + 12544)
        u = place("u", [P, 2, NT, 4], F32, at_v + 12928)
        cnt16 = place("cnt16", [P, 2, 16], F32, at_v + 13184)
        masks = place("masks", [P, 6, NT], F32, at_v + 13312)
        onehot = place("onehot", [P, 2, NT, 16], F32, at_v + 13568)
        PS = ctx.enter_context(nc.psum_tensor("PS", [P, BANKS, HALF], F32))

        job_full = sem("job_full")
        job_act = sem("job_act")
        job_done = sem("job_done")
        raw_full = [sem("raw_full0"), sem("raw_full1")]
        squared = sem("squared")
        hidden = sem("hidden")
        qexp_done = sem("qexp_done")
        hi_done = sem("hi_done")
        lo_done = sem("lo_done")
        scaled = sem("scaled")
        raw_added = sem("raw_added")
        x_loaded = sem("x_loaded")
        params_loaded = sem("params_loaded")
        nibble_loaded = sem("nibble_loaded")
        row_loaded = [sem(f"row_loaded{i}") for i in range(3)]
        consts = sem("consts")
        var_ready = sem("var_ready")
        std_ready = sem("std_ready")
        ln_ready = sem("ln_ready")
        dchain = sem("dchain")
        pchain = sem("pchain")
        achain = sem("achain")
        hg_stored = sem("hg_stored")
        keys_ready = sem("keys_ready")
        trash_zeroed = sem("trash_zeroed")
        key_stored = sem("key_stored")
        edge_loaded = sem("edge_loaded")
        zeroed = sem("zeroed")
        edge_row = sem("edge_row")
        edge_row_free = sem("edge_row_free")
        edge_ready = sem("edge_ready")
        added = [sem("added_w"), sem("added_c")]
        proj_loaded = sem("proj_loaded")
        vsum_ready = sem("vsum_ready")
        kmax_ready = sem("kmax_ready")
        kmax_all = sem("kmax_all")
        nkmax_ready = sem("nkmax_ready")
        kexp_done = sem("kexp_done")
        wg_ready = sem("wg_ready")
        copied = sem("copied")
        xs_ready = sem("xs_ready")
        deg_read = sem("deg_read")
        u_ready = sem("u_ready")
        out_ready = sem("out_ready")
        out_stored = sem("out_stored")

        block = ctx.enter_context(nc.Block())
        ROWS = ["bv0", "bo0", "b20", "bv1", "bo1", "b21", "fc_b", "b_1", "b_2"]
        row_src = {"fc_b": a["L1_gnn_fc_b"], "b_1": a["L1_gnn_b_1"], "b_2": a["L1_gnn_b_2"]}
        for l in range(DEPTH):
            row_src[f"bv{l}"] = a["L0_mix_bv"][l]
            row_src[f"bo{l}"] = a["L0_mix_bo"][l]
            row_src[f"b2{l}"] = a["L0_mix_b2"][l]
        row_at = {name: i for i, name in enumerate(ROWS)}

        def raw_wait(eng, name):
            r = raw_no[name]
            eng.wait_ge(raw_full[r % 2], 16 * (r // 2 + 1))

        @block.sync
        def _(sp):
            for t in range(NT):
                sp.dma_start(X[:, t, :], x_in[t * P:(t + 1) * P, :]).then_inc(x_loaded, 16)

            def free_raw(r):
                b = blocks[r - 2]
                if b.kind in ("slot", "operand"):
                    sp.wait_ge(lo_done, split_no[b.name] + 1)
                elif b.kind in ("transpose", "counted"):
                    sp.wait_ge(job_full, b.last_job + 1 if b.kind == "transpose" else JOB["deg"] + 1)
                elif b.kind == "added":
                    sp.wait_ge(raw_added, 1 + int(b.name[1]))

            def load(r):
                b = blocks[r]
                if b.kind == "counted":
                    if b.name in ("deg2", "deg3"):
                        sp.wait_ge(deg_read, int(b.name[3]) - 1)
                    else:
                        free_raw(r)
                elif r >= 2 and blocks[r - 2].name in ("deg2", "deg3"):
                    sp.wait_ge(job_full, JOB["deg"] + 1)
                elif r >= 2:
                    free_raw(r)
                if b.name == "hg0":
                    sp.wait_ge(hg_stored, 16 * NT)
                if b.name == "adj0":
                    for s in added:
                        sp.wait_ge(s, 16 * EC)
                n = b.source.shape[1]
                sp.dma_start(raw[:, r % 2, :].rearrange("p (k n) -> p k n", k=n), b.source).then_inc(raw_full[r % 2], 16)

            first_e, per_e = raw_no["e0.w1.0"], 3 * FB
            store_at = raw_no["gnn_w"] + 3
            for r in range(first_e):
                load(r)
                if r == store_at:
                    for t in range(NT):
                        sp.wait_ge(job_act, ACTS[JOB["hg"] + t])
                        sp.dma_start(hg_dram[t * P:(t + 1) * P, :], G[:, t, :]).then_inc(hg_stored, 16)
            with sp.Fori(0, EXPERTS) as e:
                for k in range(per_e):
                    fb, which = k // 3, k % 3
                    src = a[("L0_ffn_w1", "L0_ffn_w3", "L0_ffn_w2")[which]][bass.ds(e, 1)]
                    if which == 2:
                        src = src[:, fb * D:(fb + 1) * D, :].rearrange("o (k p) n -> p (o k) n", p=P)
                    else:
                        src = src[:, :, fb * D:(fb + 1) * D].rearrange("o (k p) n -> p (o k) n", p=P)
                    sp.wait_ge(lo_done, split_no["e0.w1.0"] + per_e * e + k - 1)
                    r = first_e + k
                    sp.dma_start(raw[:, r % 2, :].rearrange("p (k n) -> p k n", k=NK), src).then_inc(raw_full[r % 2], 16)
            for r in range(first_e + per_e * EXPERTS, len(blocks)):
                load(r)
            sp.wait_ge(out_ready, 1)
            for t in range(NT):
                sp.dma_start(out[t * P:(t + 1) * P, :], X[:, t, :]).then_inc(out_stored, 16)
            sp.wait_ge(out_stored, 16 * NT)

        @block.tensor
        def _(pe):
            def bank(n):
                return PS[:, n % BANKS, :]

            def open_job(n, e=0):
                if n >= BANKS and "D" in WHO[n - BANKS]:
                    pe.wait_ge(job_done, DONES[n - BANKS] + DONES_PER_EXPERT * e)
                elif n >= BANKS:
                    pe.wait_ge(job_act, ACTS[n - BANKS] + ACTS_PER_EXPERT * e)

            def evacuated(stage, count):
                n = JOB[stage] + count - 1
                if "D" in WHO[n]:
                    pe.wait_ge(job_done, DONES[n])
                else:
                    pe.wait_ge(job_act, ACTS[n])

            def split_mm(ps, lhs_hi, lhs_lo, rhs_hi, rhs_lo, start, stop):
                pe.matmul(ps, lhs_hi, rhs_hi, start=start, stop=False)
                pe.matmul(ps, lhs_hi, rhs_lo, start=False, stop=False)
                return pe.matmul(ps, lhs_lo, rhs_hi, start=False, stop=stop)

            def w_wait(name):
                pe.wait_ge(lo_done, split_no[name] + 1)

            def feature_job(n, act, s, m, c, e=0):
                open_job(n, e)
                for k in range(NK):
                    w = slice(k * D + m * P, k * D + m * P + P)
                    t = slice(k * N + c * HALF, k * N + c * HALF + HALF)
                    mm = split_mm(bank(n), W[:, s, 0, w], W[:, s, 1, w], act[:, 0, t], act[:, 1, t], k == 0, k == NK - 1)
                mm.then_inc(job_full, 1)

            def token_mms(n, act, s, t, start=True, stop=True):
                for k in range(NK):
                    w = slice(k * D, (k + 1) * D)
                    x = slice(k * N + t * P, k * N + t * P + P)
                    mm = split_mm(bank(n), act[:, 0, x], act[:, 1, x], W[:, s, 0, w], W[:, s, 1, w],
                                  start and k == 0, stop and k == NK - 1)
                return mm

            def token_job(n, act, s, t, e=0):
                open_job(n, e)
                token_mms(n, act, s, t).then_inc(job_full, 1)

            def table_job(n, act, s, half):
                open_job(n)
                for r in range(NT):
                    w = slice(r * 256 + half * P, r * 256 + half * P + P)
                    x = slice(r * D, (r + 1) * D)
                    mm = split_mm(bank(n), W[:, s, 0, w], W[:, s, 1, w], act[:, 0, x], act[:, 1, x], r == 0, r == NT - 1)
                mm.then_inc(job_full, 1)

            def transpose_job(n, src, c, j):
                open_job(n)
                for q in range(4):
                    mm = pe.transpose(bank(n)[:, q * P:(q + 1) * P], src[:, 4 * c + q, j * P:(j + 1) * P], ident[:, :])
                mm.then_inc(job_full, 1)

            def weight_transpose(stage, name):
                raw_wait(pe, name)
                rb = raw_no[name] % 2
                for k in range(NK):
                    n = JOB[stage] + k
                    open_job(n)
                    for q in range(NK):
                        mm = pe.transpose(bank(n)[:, q * P:(q + 1) * P], raw[:, rb, q * D + k * P:q * D + (k + 1) * P], ident[:, :])
                    mm.then_inc(job_full, 1)

            def all_transposes(stage, src, ready, count):
                for c in range(2):
                    pe.wait_ge(ready, count + c)
                    for j in range(NK):
                        transpose_job(JOB[stage] + 4 * c + j, src, c, j)

            pe.wait_ge(consts, 1)
            all_transposes("xn_T", X, ln_ready, 1)
            weight_transpose("gnn_w_T", "gnn_w")
            evacuated("gnn_w_T", 4)
            for t in range(NT):
                token_job(JOB["hg"] + t, op_a, slot_of["gnn_w"] % SLOTS, t)
            pe.wait_ge(keys_ready, 1)
            n = JOB["edge_T"]
            open_job(n)
            for q in range(3):
                mm = pe.transpose(bank(n)[:, q * P:(q + 1) * P], edge_f[:, 2 + q, :], ident[:, :])
            mm.then_inc(job_full, 1)

            for l in range(DEPTH):
                all_transposes(f"y_T{l}", G, ln_ready, 3 + 4 * l)
                n = JOB[f"proj{l}"]
                pe.wait_ge(proj_loaded, 64 * (l + 1))
                open_job(n)
                for i in range(2):
                    mm = pe.transpose(bank(n)[:, i * P:(i + 1) * P], proj_nat[:, i, :, :].rearrange("p a d -> p (a d)"), ident[:, :])
                mm.then_inc(job_full, 1)
                evacuated(f"y_T{l}", 8)
                for i, (x, w) in enumerate((("q", "wq"), ("k", "wk"))):
                    w_wait(f"{w}{l}")
                    for j in range(8):
                        feature_job(JOB[f"{x}{l}"] + j, op_a, slot_of[f"{w}{l}"] % SLOTS, j // 2, j % 2)
                    n = JOB[f"d{x}{l}"]
                    pe.wait_ge(squared, 16 * l + 8 * i + 8)
                    open_job(n)
                    for t in range(NT):
                        for m in range(NK):
                            at = slice((t % 4) * P, (t % 4 + 1) * P)
                            mm = pe.matmul(bank(n)[:, t * HEADS + 2 * m:t * HEADS + 2 * m + 2], G[:, 2 * m + t // 4, at],
                                           head_sel[:, :], start=True, stop=True)
                    mm.then_inc(job_full, 1)
                w_wait(f"wv{l}")
                for t in range(NT):
                    token_job(JOB[f"v{l}"] + t, op_a, slot_of[f"wv{l}"] % SLOTS, t)
                n = JOB[f"vsum{l}"]
                evacuated(f"v{l}", 8)
                open_job(n)
                for t in range(NT):
                    mm = pe.matmul(bank(n), eps_ones[:, :], G[:, t, :], start=(t == 0), stop=(t == NT - 1))
                mm.then_inc(job_full, 1)
                for hp in range(HEADS // 2):
                    s = f"{l}.{hp}"
                    for x, feat in (("kd", k_T), ("qd", q_T)):
                        for t in range(NT):
                            n = JOB[x + s] + t
                            open_job(n)
                            pe.matmul(bank(n), feat[:, hp, t * P:(t + 1) * P], proj[:, :, :].rearrange("p a m -> p (a m)"),
                                      start=True, stop=True).then_inc(job_full, 1)

                    def turn(t):
                        n = JOB[("eT_a" if t < 4 else "eT_b") + s] + t % 4
                        pe.wait_ge(qexp_done, 32 * l + 8 * hp + t + 1)
                        open_job(n)
                        for q in range(4):
                            mm = pe.transpose(bank(n)[:, q * P:(q + 1) * P], G[:, t, q * P:(q + 1) * P], ident[:, :])
                        mm.then_inc(job_full, 1)

                    def attend(t):
                        n = JOB[("o_a" if t < 4 else "o_b") + s] + t % 4
                        evacuated(("eT_a" if t < 4 else "eT_b") + s, t % 4 + 1)
                        open_job(n)
                        for h in range(2):
                            for mh in range(2):
                                mm = pe.matmul(bank(n)[:, h * VW:(h + 1) * VW], E_T[:, t % 4, 2 * h + mh, :],
                                               ctx_sb[:, 2 * h + mh, :], start=(mh == 0), stop=(mh == 1))
                        mm.then_inc(job_full, 1)

                    for t in range(4):
                        turn(t)
                    n = JOB["ctx" + s]
                    open_job(n)
                    for h in range(2):
                        pe.wait_ge(kexp_done, 2 * (4 * l + hp) + h + 1)
                        for mh in range(2):
                            for t in range(NT):
                                mm = pe.matmul(bank(n)[:, (2 * h + mh) * VW:(2 * h + mh + 1) * VW],
                                               kd[:, h, t, mh * P:(mh + 1) * P], V[:, t, 2 * hp + h, :],
                                               start=(t == 0), stop=(t == NT - 1))
                    mm.then_inc(job_full, 1)
                    n = JOB["csum" + s]
                    evacuated("ctx" + s, 1)
                    open_job(n)
                    for h in range(2):
                        for mh in range(2):
                            mm = pe.matmul(bank(n)[:, h * VW:(h + 1) * VW], eps_ones[:, :], ctx_sb[:, 2 * h + mh, :],
                                           start=(mh == 0), stop=(mh == 1))
                    mm.then_inc(job_full, 1)
                    for t in range(4):
                        attend(t)
                    for t in range(4, NT):
                        turn(t)
                    for t in range(4, NT):
                        attend(t)
                for c in range(2):
                    evacuated(f"o_b{l}.3", 4)
                    for j in range(NK):
                        transpose_job(JOB[f"o_T{l}"] + 4 * c + j, o_tok, c, j)
                evacuated(f"o_T{l}", 8)
                w_wait(f"wo{l}")
                for t in range(NT):
                    token_job(JOB[f"wo{l}"] + t, op_b, slot_of[f"wo{l}"] % SLOTS, t)
                all_transposes(f"y2_T{l}", G, ln_ready, 5 + 4 * l)
                evacuated(f"y2_T{l}", 8)
                for fb in range(MLP):
                    w_wait(f"up{l}.{fb}")
                    for j in range(8):
                        feature_job(JOB[f"up{l}.{fb}"] + j, op_a, slot_of[f"up{l}.{fb}"] % SLOTS, j // 2, j % 2)
                    w_wait(f"down{l}.{fb}")
                    pe.wait_ge(hidden, 8 * (MLP * l + fb) + 8)
                    for t in range(NT):
                        token_job(JOB[f"down{l}.{fb}"] + t, op_b, slot_of[f"down{l}.{fb}"] % SLOTS, t)

            pe.wait_ge(lo_done, split_no["hg1"] + 1)
            for t in range(NT):
                w_wait(f"adj{t // 2}")
                table_job(JOB["gnn"] + t, op_a, slot_of[f"adj{t // 2}"] % SLOTS, t % 2)
            all_transposes("xt_T", G, ln_ready, 4 * DEPTH + 3)
            evacuated("xt_T", 8)
            pe.wait_ge(wg_ready, 1)
            n = JOB["gate"]
            open_job(n)
            for t in range(NT):
                for k in range(NK):
                    x = slice(k * N + t * P, k * N + t * P + P)
                    mm = split_mm(bank(n)[:, t * EXPERTS:(t + 1) * EXPERTS], op_a[:, 0, x], op_a[:, 1, x],
                                  wg[:, 0, k, :], wg[:, 1, k, :], k == 0, k == NK - 1)
            mm.then_inc(job_full, 1)

            with pe.Fori(0, EXPERTS) as e:
                for fb in range(FB):
                    base = JOB["experts"] + 24 * fb
                    s1, s3, s2 = ((slot_of["e0.w1.0"] + 3 * fb + i) % SLOTS for i in range(3))
                    w = split_no["e0.w1.0"] + 3 * fb
                    pe.wait_ge(lo_done, w + 2 + 3 * FB * e)
                    for j in range(8):
                        feature_job(base + 2 * j, op_a, s1, j // 2, j % 2, e)
                        feature_job(base + 2 * j + 1, op_a, s3, j // 2, j % 2, e)
                    pe.wait_ge(lo_done, w + 3 + 3 * FB * e)
                    pe.wait_ge(job_done, DONES[base + 15] + DONES_PER_EXPERT * e)
                    for t in range(NT):
                        token_job(base + 16 + t, op_b, s2, t, e)

            all_transposes("x3_T", G, ln_ready, 4 * DEPTH + 5)
            n = JOB["deg"]
            open_job(n)
            for q in range(4):
                raw_wait(pe, f"deg{q}")
                rb = raw_no[f"deg{q}"] % 2
                for half in range(2):
                    t = 2 * q + half
                    for r in range(NT):
                        at = slice(r * 256 + half * P, r * 256 + half * P + P)
                        mm = pe.matmul(bank(n)[:, t:t + 1], raw[:, rb, at], ones[:, 0:1], start=(r == 0), stop=(r == NT - 1))
                if q < 3:
                    mm.then_inc(deg_read, 1)
            mm.then_inc(job_full, 1)
            weight_transpose("wv_T", "l1_wv")
            evacuated("wv_T", 4)
            for t in range(NT):
                token_job(JOB["xwv"] + t, op_a, slot_of["l1_wv"] % SLOTS, t)
            weight_transpose("wth_T", "l1_wth")
            evacuated("wth_T", 4)
            for t in range(NT):
                token_job(JOB["theta"] + t, op_a, slot_of["l1_wth"] % SLOTS, t)
            evacuated("theta", 8)
            for m in range(NK):
                n = JOB["kv"] + m
                open_job(n)
                for t in range(NT):
                    mm = pe.matmul(bank(n), theta[:, t, m * P:(m + 1) * P], xwv[:, t, :], start=(t == 0), stop=(t == NT - 1))
                mm.then_inc(job_full, 1)
            n = JOB["mean"]
            open_job(n)
            for t in range(NT):
                mm = pe.matmul(bank(n), ones[:, :], xwv[:, t, :], start=(t == 0), stop=(t == NT - 1))
            mm.then_inc(job_full, 1)
            evacuated("kv", 4)
            for t in range(NT):
                token_job(JOB["xkv"] + t, op_a, slot_of["kv"] % SLOTS, t)
            weight_transpose("fc_T", "l1_fc")
            evacuated("fc_T", 4)
            for t in range(NT):
                token_job(JOB["h"] + t, op_a, slot_of["l1_fc"] % SLOTS, t)
            for c in range(2):
                evacuated("h", 8)
                for j in range(NK):
                    transpose_job(JOB["h_T"] + 4 * c + j, G, c, j)
            for g in range(2):
                pe.wait_ge(xs_ready, g + 1)
                for t in range(NT):
                    w_wait(f"cnt{g}.{t // 2}")
                    table_job(JOB[f"agg{g}"] + t, op_b, slot_of[f"cnt{g}.{t // 2}"] % SLOTS, t % 2)
                for c in range(2):
                    evacuated(f"agg{g}", 8)
                    for j in range(NK):
                        transpose_job(JOB[f"f_T{g}"] + 4 * c + j, G, c, j)
                evacuated(f"f_T{g}", 8)
                w_wait(f"gw1.{g}")
                w_wait(f"gw2.{g}")
                for t in range(NT):
                    n = JOB[f"rst{g}"] + t
                    open_job(n)
                    token_mms(n, op_b, slot_of[f"gw1.{g}"] % SLOTS, t, True, False)
                    token_mms(n, op_a, slot_of[f"gw2.{g}"] % SLOTS, t, False, True).then_inc(job_full, 1)

            pe.wait_ge(u_ready, 1)
            for j in range(4):
                n = JOB["u_T"] + j
                open_job(n)
                for q in range(4):
                    mm = pe.transpose(bank(n)[0:4, q * P:(q + 1) * P], u[:, j // 2, 4 * (j % 2) + q, :], ident[:, :])
                mm.then_inc(job_full, 1)
            pe.wait_ge(nibble_loaded, 16 * PARAMS_NIBBLE)
            for p in range(2):
                n = JOB["w1_T"] + p
                open_job(n)
                pe.transpose(bank(n)[:, 0:P], wn_a[:, p, 0:P], ident[:, :])
                pe.transpose(bank(n)[:, P:GE], wn_b[:, p, 0:P], ident[0:GE_LO, 0:GE_LO])
                pe.transpose(bank(n)[0:GE_LO, GE:GE + P], wn_a[:, p, P:GE], ident[:, :])
                pe.transpose(bank(n)[0:GE_LO, GE + P:2 * GE], wn_b[:, p, P:GE], ident[0:GE_LO, 0:GE_LO])\
                    .then_inc(job_full, 1)
            evacuated("w1_T", 2)
            for i in range(8):
                p, pos, c = i // 4, i // 2 % 2, i % 2
                base = JOB["alu"] + 5 * i
                b2 = 2 * (i % 2)
                tok = slice(c * HALF, (c + 1) * HALF)
                open_job(base)
                pe.matmul(bank(base), w0_T[:, p, 0:P], u_T[:, pos, tok], start=True, stop=True).then_inc(job_full, 1)
                open_job(base + 1)
                pe.matmul(bank(base + 1)[0:GE_LO, :], w0_T[:, p, P:GE], u_T[:, pos, tok], start=True, stop=True)\
                    .then_inc(job_full, 1)
                pe.wait_ge(job_act, ACTS[base + 1])
                for m, rows_m in ((0, slice(0, P)), (1, slice(P, GE))):
                    n = base + 2 + m
                    M = rows_m.stop - rows_m.start
                    open_job(n)
                    pe.matmul(bank(n)[0:M, :], w1_T[:, p, 0, rows_m], h1[:, b2, :], start=True, stop=False)
                    pe.matmul(bank(n)[0:M, :], w1_T[0:GE_LO, p, 1, rows_m], h1[0:GE_LO, b2 + 1, :], start=False, stop=True)\
                        .then_inc(job_full, 1)
                pe.wait_ge(job_act, ACTS[base + 3])
                n = base + 4
                open_job(n)
                for q in range(4):
                    at = slice(q * P, (q + 1) * P)
                    pe.matmul(bank(n)[:, 2 * q:2 * q + 2], h2[:, b2, at], w2_T[:, p, 0, :], start=True, stop=False)
                    mm = pe.matmul(bank(n)[:, 2 * q:2 * q + 2], h2[0:GE_LO, b2 + 1, at], w2_T[0:GE_LO, p, 1, :],
                                   start=False, stop=True)
                mm.then_inc(job_full, 1)

        @block.scalar
        def _(act):
            def bank(n):
                return PS[:, n % BANKS, :]

            def ask_row(name, after_job):
                if after_job is not None:
                    act.wait_ge(job_done, DONES[after_job])
                act.dma_start(rowv[:, row_at[name] % 3, :], row_src[name].partition_broadcast(P)).then_inc(row_loaded[row_at[name] % 3], 16)

            def split_hi(name):
                s = slot_of[name]
                if s >= SLOTS:
                    act.wait_ge(job_full, slot_last_job[slot_order[s - SLOTS]] + 1)
                if name.startswith("gw"):
                    act.wait_ge(scaled, 2 * int(name[4]) + int(name[2]))
                raw_wait(act, name)
                act.activation(W[:, s % SLOTS, 0, :], raw[:, raw_no[name] % 2, :], ACT.Copy).then_inc(hi_done, 1)

            def ln_sqrt(i, c):
                act.wait_ge(var_ready, i)
                act.activation(sd[:, 4 * c:4 * c + 4], mv[:, 4 * c:4 * c + 4, 1], ACT.Sqrt, bias=lneps[:, :])\
                    .then_inc(std_ready, 1)

            def hi_transposed(stage, op, scale=1.0, bias=0.0):
                for c in range(2):
                    for j in range(NK):
                        n = JOB[stage] + 4 * c + j
                        act.wait_ge(job_full, n + 1)
                        dst = op[:, 0, j * N + c * HALF:j * N + (c + 1) * HALF]
                        if scale is None:
                            act.activation(dst, bank(n), ACT.Identity, scale=bias[0][:, j:j + 1], bias=bias[1][:, j:j + 1])\
                               .then_inc(job_act, 1)
                        else:
                            act.activation(dst, bank(n), ACT.Copy).then_inc(job_act, 1)

            def hi_slot(stage, name):
                s = slot_of[name]
                if s >= SLOTS:
                    act.wait_ge(job_full, slot_last_job[slot_order[s - SLOTS]] + 1)
                for k in range(NK):
                    n = JOB[stage] + k
                    act.wait_ge(job_full, n + 1)
                    act.activation(W[:, s % SLOTS, 0, k * D:(k + 1) * D], bank(n), ACT.Copy).then_inc(job_act, 1)

            for l in range(DEPTH):
                at = 0
                for name, cols in (("ln1_g", 4), ("ln1_b", 4), ("bq", 4), ("bk", 4), ("ln2_g", 4), ("ln2_b", 4), ("b1", 16)):
                    act.dma_start(colv[:, l, at:at + cols], a["L0_mix_" + name][l].rearrange("(j p) -> p j", p=P))\
                        .then_inc(params_loaded, 16)
                    at += cols
            act.dma_start(wg_raw[:, :, :], a["L0_ffn_wg"].rearrange("(k p) e -> p k e", p=P)).then_inc(params_loaded, 16)
            act.dma_start(bg[:, :], a["L0_ffn_bg"].partition_broadcast(P)).then_inc(params_loaded, 16)
            for i in range(3):
                ask_row(ROWS[i], None)
            act.wait_ge(params_loaded, 16 * PARAMS_MIX)
            act.wait_ge(consts, 1)
            for c in range(2):
                ln_sqrt(1 + c, c)
            hi_transposed("xn_T", op_a)
            hi_slot("gnn_w_T", "gnn_w")
            split_hi("wq0")
            for t in range(NT):
                n = JOB["hg"] + t
                act.wait_ge(job_full, n + 1)
                act.activation(G[:, t, :], bank(n), ACT.Copy).then_inc(job_act, 1)
            for c in range(2):
                ln_sqrt(3 + c, c)
            for l in range(DEPTH):
                hi_transposed(f"y_T{l}", op_a, None, (colv[:, l, 0:4], colv[:, l, 4:8]))
                n = JOB[f"proj{l}"]
                act.wait_ge(job_full, n + 1)
                act.activation(proj[0:DH, 0, :], bank(n)[0:DH, 0:NBF], ACT.Copy, scale=NORMALIZER)
                act.activation(proj[DH:P, 1, :], bank(n)[DH:P, 0:NBF], ACT.Copy, scale=NORMALIZER).then_inc(job_act, 1)
                split_hi(f"wk{l}")
                for i, (x, dst) in enumerate((("q", q_T), ("k", k_T))):
                    for j in range(8):
                        n = JOB[f"{x}{l}"] + j
                        m, c = j // 2, j % 2
                        act.wait_ge(job_full, n + 1)
                        act.activation(dst[:, m, c * HALF:(c + 1) * HALF], bank(n), ACT.Identity,
                                       bias=colv[:, l, 8 + 4 * i + m:9 + 4 * i + m]).then_inc(job_act, 1)
                        if j == 3:
                            split_hi(f"wv{l}" if i == 0 else f"wo{l}")
                    n = JOB[f"d{x}{l}"]
                    act.wait_ge(job_full, n + 1)
                    act.activation(dexp[:, i, :, :].rearrange("p t h -> p (t h)"), bank(n)[:, 0:NT * HEADS], ACT.Exp,
                                   scale=-1.0).then_inc(job_act, 1)
                split_hi(f"up{l}.0")
                n = JOB[f"vsum{l}"]
                act.wait_ge(job_full, n + 1)
                act.activation(vsum[:, :, 0:DH], bank(n).rearrange("p (h d) -> p h d", h=HEADS), ACT.Copy).then_inc(job_act, 1)
                for hp in range(HEADS // 2):
                    s = f"{l}.{hp}"
                    for t in range(NT):
                        n = JOB["kd" + s] + t
                        act.wait_ge(job_full, n + 1)
                        act.activation(kd[:, :, t, :], bank(n).rearrange("p (h m) -> p h m", h=2), ACT.Copy).then_inc(job_act, 1)

                    def query_exp(t):
                        n = JOB["qd" + s] + t
                        act.wait_ge(job_done, DONES[n])
                        act.activation(G[:, t, :], G[:, t, :], ACT.Exp).then_inc(qexp_done, 1)

                    for t in range(4):
                        query_exp(t)
                    act.wait_ge(nkmax_ready, 4 * l + hp + 1)
                    for h in range(2):
                        act.activation(kd[:, h, :, :], kd[:, h, :, :], ACT.Exp, bias=nkmax[:, h:h + 1]).then_inc(kexp_done, 1)
                    for t in range(4, NT):
                        query_exp(t)
                    n = JOB["csum" + s]
                    act.wait_ge(job_full, n + 1)
                    act.activation(csum[:, :, :].rearrange("p h d -> p (h d)"), bank(n)[:, 0:2 * VW], ACT.Copy).then_inc(job_act, 1)
                hi_transposed(f"o_T{l}", op_b)
                split_hi(f"down{l}.0")
                ln_sqrt(5 + 4 * l, 0)
                ln_sqrt(6 + 4 * l, 1)
                hi_transposed(f"y2_T{l}", op_a, None, (colv[:, l, 16:20], colv[:, l, 20:24]))
                for fb in range(MLP):
                    for j in range(8):
                        n = JOB[f"up{l}.{fb}"] + j
                        m = fb * 4 + j // 2
                        act.wait_ge(job_full, n + 1)
                        act.activation(G[:, j, :], bank(n), ACT.Gelu, bias=colv[:, l, 24 + m:25 + m]).then_inc(job_act, 1)
                        if j == 3 and fb + 1 < MLP:
                            split_hi(f"up{l}.{fb + 1}")
                    if fb + 1 < MLP:
                        split_hi(f"down{l}.{fb + 1}")
                    elif l + 1 < DEPTH:
                        split_hi(f"wq{l + 1}")
                        ask_row(ROWS[3], JOB["down0.0"])
                        ask_row(ROWS[4], JOB["down0.0"])
                    if fb + 1 == MLP:
                        if l + 1 < DEPTH:
                            ln_sqrt(7 + 4 * l, 0)
                        if l + 1 < DEPTH:
                            ln_sqrt(8 + 4 * l, 1)
                            ask_row(ROWS[5], JOB["down0.3"] + 7)
            LN1 = 4 * DEPTH + 3
            for h in range(2):
                act.wait_ge(job_full, JOB["up1.3"] + 8)
                raw_wait(act, f"hg{h}")
                act.activation(op_a[:, 0, h * BLK:(h + 1) * BLK], raw[:, raw_no[f"hg{h}"] % 2, :], ACT.Copy).then_inc(hi_done, 1)
            for i in range(3):
                ask_row(ROWS[6 + i], JOB["down1.3"] + 7)
            for q in range(3):
                split_hi(f"adj{q}")
            split_hi("adj3")
            ln_sqrt(LN1, 0)
            split_hi("e0.w1.0")
            ln_sqrt(LN1 + 1, 1)
            split_hi("e0.w3.0")
            hi_transposed("xt_T", op_a)
            n = JOB["gate"]
            for i in range(3):
                act.wait_ge(copied, i + 1)
                act.activation(g8[:, i + 1, :, :].rearrange("p t e -> p (t e)"), g8[:, i + 1, :, :].rearrange("p t e -> p (t e)"),
                               ACT.Exp).then_inc(achain, 1)

            def expert(e, last):
                sh = JOBS_PER_EXPERT * e
                per = 3 * FB

                def conv(k, nxt=0):
                    s = slot_of["e0.w1.0"] + k
                    r = raw_no["e0.w1.0"] + k
                    kk = (k - 3) % per
                    job = JOB["experts"] + 24 * (kk // 3) + (15 if kk % 3 < 2 else 23) - (JOBS_PER_EXPERT if k < 3 else 0)
                    act.wait_ge(job_full, job + 1 + JOBS_PER_EXPERT * nxt + sh)
                    act.wait_ge(raw_full[r % 2], 16 * (r // 2 + 1 + per // 2 * nxt) + 16 * (per // 2) * e)
                    act.activation(W[:, s % SLOTS, 0, :], raw[:, r % 2, :], ACT.Copy).then_inc(hi_done, 1)

                for fb in range(FB):
                    base = JOB["experts"] + 24 * fb
                    for j in range(8):
                        n = base + 2 * j
                        act.wait_ge(job_full, n + 1 + sh)
                        act.activation(G[:, j, :], bank(n), ACT.Gelu).then_inc(job_act, 1)
                        if j == 1:
                            conv(3 * fb + 2)
                    if fb + 1 < FB:
                        conv(3 * fb + 3)
                        conv(3 * fb + 4)
                    elif not last:
                        conv(0, 1)
                        conv(1, 1)
                    if last and fb + 1 == FB:
                        ln_sqrt(LN1 + 2, 0)
                    if last and fb + 1 == FB:
                        ln_sqrt(LN1 + 3, 1)

            with act.Fori(0, EXPERTS - 1) as e:
                expert(e, False)
            expert(EXPERTS - 1, True)
            hi_transposed("x3_T", op_a)
            n = JOB["deg"]
            act.wait_ge(job_done, DONES[n])
            act.activation(norm[:, :], norm[:, :], ACT.Sqrt).then_inc(achain, 1)
            hi_slot("wv_T", "l1_wv")
            for t in range(NT):
                n = JOB["xwv"] + t
                act.wait_ge(job_full, n + 1)
                act.activation(xwv[:, t, :], bank(n), ACT.Copy).then_inc(job_act, 1)
            hi_slot("wth_T", "l1_wth")
            for t in range(NT):
                n = JOB["theta"] + t
                act.wait_ge(job_full, n + 1)
                act.activation(theta[:, t, :], bank(n), ACT.Copy).then_inc(job_act, 1)
            hi_slot("kv", "kv")
            n = JOB["mean"]
            act.wait_ge(job_full, n + 1)
            act.activation(mean_row[:, :], bank(n), ACT.Copy, scale=1.0 / N).then_inc(job_act, 1)
            hi_slot("fc_T", "l1_fc")
            split_hi("cnt0.0")
            split_hi("cnt0.1")
            hi_transposed("h_T", op_a)
            for g in range(2):
                if g == 0:
                    split_hi("cnt0.2")
                split_hi(f"cnt{g}.3")
                split_hi(f"gw1.{g}")
                split_hi(f"gw2.{g}")
                hi_transposed(f"f_T{g}", op_b)
                if g == 0:
                    split_hi("cnt1.0")
                    split_hi("cnt1.1")
                    split_hi("cnt1.2")
                else:
                    ln_sqrt(LN1 + 4, 0)
                    ln_sqrt(LN1 + 5, 1)
            for i in range(8):
                p = i // 4
                base = JOB["alu"] + 5 * i
                b2 = 2 * (i % 2)
                for layer, dst in ((0, h1), (1, h2)):
                    for m, M in ((0, P), (1, GE_LO)):
                        n = base + 2 * layer + m
                        act.wait_ge(job_full, n + 1)
                        act.activation(dst[0:M, b2 + m, :], bank(n)[0:M, :], ACT.Relu, bias=b_hid[0:M, p, layer, m:m + 1])\
                            .then_inc(job_act, 1)

        @block.vector
        def _(dve):
            def bank(n):
                return PS[:, n % BANKS, :]

            count = [0]

            def link(ins, loop=0):
                count[0] += 1
                ins.then_inc(dchain, 1)
                dve.wait_ge(dchain, count[0] + loop)

            def layer_norm(i, c, dst):
                for q in range(4):
                    ins = dve.bn_stats(stats[:, q, :], X[:, 4 * c + q, :])
                link(ins)
                for q in range(4):
                    ins = dve.bn_aggr(mv[:, 4 * c + q, :], stats[:, q, :])
                ins.then_inc(var_ready, 1)
                dve.wait_ge(std_ready, i)
                link(dve.reciprocal(rstd[:, 4 * c:4 * c + 4], sd[:, 4 * c:4 * c + 4]))
                for q in range(4):
                    t = 4 * c + q
                    ins = dve.tensor_scalar(dst[:, t, :], X[:, t, :], mv[:, t, 0:1], rstd[:, t:t + 1], ALU.subtract, ALU.mult)
                ins.then_inc(ln_ready, 1)

            def lo_transposed(stage, op, gb=None):
                for c in range(2):
                    for j in range(NK):
                        n = JOB[stage] + 4 * c + j
                        at = slice(j * N + c * HALF, j * N + (c + 1) * HALF)
                        if gb is not None:
                            dve.wait_ge(job_act, ACTS[n])
                            link(dve.tensor_scalar(tmp[:, j % 2, :], bank(n), gb[0][:, j:j + 1], gb[1][:, j:j + 1], ALU.mult, ALU.add))
                            dve.tensor_tensor(op[:, 1, at], tmp[:, j % 2, :], op[:, 0, at].bitcast(F32), ALU.subtract).then_inc(job_done, 1)
                        else:
                            dve.wait_ge(job_act, ACTS[n])
                            dve.tensor_tensor(op[:, 1, at], bank(n), op[:, 0, at].bitcast(F32), ALU.subtract).then_inc(job_done, 1)

            def lo_slot(stage, name):
                s = slot_of[name] % SLOTS
                for k in range(NK):
                    n = JOB[stage] + k
                    at = slice(k * D, (k + 1) * D)
                    dve.wait_ge(job_act, ACTS[n])
                    dve.tensor_tensor(W[:, s, 1, at], bank(n), W[:, s, 0, at].bitcast(F32), ALU.subtract).then_inc(job_done, 1)

            def row_wait(name):
                dve.wait_ge(row_loaded[row_at[name] % 3], 16 * (row_at[name] // 3 + 1))

            def edge_batch(b):
                cs = slice(b * EB, (b + 1) * EB)
                dve.wait_ge(edge_row, 32 * (b + 1))
                link(dve.tensor_tensor(same[:, :, :], key_row[:, :, :], keycols[:, 0, cs].unsqueeze(2).to_broadcast([P, EB, P]),
                                       ALU.is_equal))
                link(dve.tensor_tensor(picked[:, :, :], same[:, :, :], w_row[:, :, :], ALU.mult))
                dve.tensor_reduce(edge_add[:, 0, cs], picked[:, :, :], AX_X, ALU.add).then_inc(edge_row_free, 1)
                link(dve.tensor_reduce(edge_add[:, 1, cs], same[:, :, :], AX_X, ALU.add))
                link(dve.tensor_tensor(picked[:, :, :], same[:, :, :], lower[:, :].unsqueeze(1).to_broadcast([P, EB, P]), ALU.mult))
                link(dve.tensor_reduce(batch[:, 0, :], picked[:, :, :], AX_X, ALU.add))
                link(dve.tensor_scalar(batch[:, 1, :], batch[:, 0, :], 0.0, None, ALU.is_equal))
                for i in range(2):
                    ins = dve.scalar_tensor_tensor(out=batch[:, 2 + i, :], in0=keycols[:, i, cs], scalar=trash[:, :],
                                                   in1=batch[:, 1, :], op0=ALU.subtract, op1=ALU.mult)
                link(ins)
                for i in range(2):
                    ins = dve.tensor_scalar(edge_ix[:, i, cs], batch[:, 2 + i, :], trash[:, :], None, ALU.add)
                ins.then_inc(edge_ready, 1)

            dve.wait_ge(consts, 1)
            dve.wait_ge(x_loaded, 16 * NT)
            for c in range(2):
                layer_norm(1 + c, c, X)
            lo_transposed("xn_T", op_a)
            lo_slot("gnn_w_T", "gnn_w")
            dve.wait_ge(edge_loaded, 16 * 3)
            for i in range(2):
                ins = dve.tensor_copy(edge_f[:, i, :], edge_int[:, i, :])
            link(ins)
            for i in range(2):
                ins = dve.scalar_tensor_tensor(out=edge_f[:, 2 + i, :], in0=edge_f[:, 1 - i, :], scalar=float(N),
                                               in1=edge_f[:, i, :], op0=ALU.mult, op1=ALU.add)
            ins.then_inc(keys_ready, 1)
            n = JOB["edge_T"]
            dve.wait_ge(job_full, n + 1)
            dve.tensor_copy(keycols[:, :, :].rearrange("p a c -> p (a c)"), bank(n)[:, 0:3 * P]).then_inc(job_done, 1)
            dve.wait_ge(hg_stored, 16 * NT)
            for c in range(2):
                layer_norm(3 + c, c, G)

            for l in range(DEPTH):
                lo_transposed(f"y_T{l}", op_a, (colv[:, l, 0:4], colv[:, l, 4:8]))
                for i, (x, src) in enumerate((("q", q_T), ("k", k_T))):
                    for j in range(8):
                        n = JOB[f"{x}{l}"] + j
                        at = src[:, j // 2, (j % 2) * HALF:(j % 2 + 1) * HALF]
                        dve.wait_ge(job_act, ACTS[n])
                        if i == 1 and j == 0:
                            dve.wait_ge(job_full, JOB[f"dq{l}"] + 1)
                        dve.tensor_tensor(G[:, j, :], at, at, ALU.mult).then_inc(squared, 1)
                row_wait(f"bv{l}")
                for t in range(NT):
                    n = JOB[f"v{l}"] + t
                    dve.wait_ge(job_full, n + 1)
                    if t == 0:
                        dve.wait_ge(job_act, ACTS[JOB[f"dk{l}"]])
                    link(dve.tensor_tensor(G[:, t, :], bank(n), rowv[:, row_at[f"bv{l}"] % 3, :], ALU.add))
                    dve.tensor_tensor(V[:, t, :, 0:DH], G[:, t, :].rearrange("p (h d) -> p h d", h=HEADS),
                                      dexp[:, 1, t, :].unsqueeze(2).to_broadcast([P, HEADS, DH]), ALU.mult)
                    dve.tensor_copy(V[:, t, :, DH], dexp[:, 1, t, :]).then_inc(job_done, 1)
                for hp in range(HEADS // 2):
                    s = f"{l}.{hp}"
                    for t in range(NT):
                        n = JOB["kd" + s] + t
                        dve.wait_ge(job_act, ACTS[n])
                        dve.tensor_reduce(kmax[:, :, t], bank(n).rearrange("p (h m) -> p h m", h=2), AX_X, ALU.max)\
                            .then_inc(job_done, 1)
                    dve.wait_ge(job_done, DONES[JOB["kd" + s] + 7])
                    dve.tensor_reduce(kmaxp[:, 0, :], kmax[:, :, :], AX_X, ALU.max).then_inc(kmax_ready, 1)
                    for t in range(NT):
                        n = JOB["qd" + s] + t
                        dve.wait_ge(job_full, n + 1)
                        link(dve.tensor_reduce(nqmax[:, t, :], bank(n).rearrange("p (h m) -> p h m", h=2), AX_X, ALU.max,
                                               negate=True))
                        if t == 0:
                            dve.wait_ge(job_full, JOB[f"vsum{l}"] + 1)
                        dve.tensor_tensor(G[:, t, :].rearrange("p (h m) -> p h m", h=2), bank(n).rearrange("p (h m) -> p h m", h=2),
                                          nqmax[:, t, :].unsqueeze(2).to_broadcast([P, 2, NBF]), ALU.add).then_inc(job_done, 1)
                        if t == 2:
                            dve.wait_ge(kmax_all, 4 * l + hp + 1)
                            dve.tensor_scalar(nkmax[:, :], kmaxp[:, 1, :], -1.0, None, ALU.mult).then_inc(nkmax_ready, 1)

                    def e_t(t):
                        n = JOB[("eT_a" if t < 4 else "eT_b") + s] + t % 4
                        dve.wait_ge(job_full, n + 1)
                        dve.tensor_copy(E_T[:, t % 4, :, :].rearrange("p q n -> p (q n)"), bank(n)).then_inc(job_done, 1)

                    def normalise(t):
                        n = JOB[("o_a" if t < 4 else "o_b") + s] + t % 4
                        dve.wait_ge(job_full, n + 1)
                        for h in range(2):
                            ins = dve.scalar_tensor_tensor(out=num[:, t % 2, h, :], in0=bank(n)[:, h * VW:(h + 1) * VW],
                                                           scalar=dexp[:, 0, t, 2 * hp + h:2 * hp + h + 1], in1=csum[:, h, :],
                                                           op0=ALU.mult, op1=ALU.add)
                        link(ins)
                        link(dve.reciprocal(rden[:, t % 2, :], num[:, t % 2, :, DH]))
                        dve.tensor_tensor(o_tok[:, t, hp * P:(hp + 1) * P].rearrange("p (h d) -> p h d", h=2), num[:, t % 2, :, 0:DH],
                                          rden[:, t % 2, :].unsqueeze(2).to_broadcast([P, 2, DH]), ALU.mult).then_inc(job_done, 1)

                    for t in range(4):
                        e_t(t)
                    n = JOB["ctx" + s]
                    dve.wait_ge(job_full, n + 1)
                    for h in range(2):
                        ins = dve.tensor_tensor(ctx_sb[:, 2 * h:2 * h + 2, :], bank(n)[:, 2 * h * VW:2 * (h + 1) * VW].rearrange("p (m d) -> p m d", m=2),
                                                vsum[:, 2 * hp + h, :].unsqueeze(1).to_broadcast([P, 2, VW]), ALU.add)
                    ins.then_inc(job_done, 1)
                    dve.wait_ge(job_act, ACTS[JOB["csum" + s]])
                    for t in range(4):
                        normalise(t)
                    for t in range(4, NT):
                        e_t(t)
                    for t in range(4, NT):
                        normalise(t)
                lo_transposed(f"o_T{l}", op_b)
                row_wait(f"bo{l}")
                for t in range(NT):
                    n = JOB[f"wo{l}"] + t
                    dve.wait_ge(job_full, n + 1)
                    link(dve.tensor_tensor(X[:, t, :], X[:, t, :], bank(n), ALU.add))
                    dve.tensor_tensor(X[:, t, :], X[:, t, :], rowv[:, row_at[f"bo{l}"] % 3, :], ALU.add).then_inc(job_done, 1)
                    if t % 4 == 3:
                        dve.wait_ge(job_done, DONES[n])
                        layer_norm(5 + 4 * l + t // 4, t // 4, G)
                lo_transposed(f"y2_T{l}", op_a, (colv[:, l, 16:20], colv[:, l, 20:24]))
                for fb in range(MLP):
                    for j in range(8):
                        n = JOB[f"up{l}.{fb}"] + j
                        m, c = j // 2, j % 2
                        at = slice(m * N + c * HALF, m * N + (c + 1) * HALF)
                        dve.wait_ge(job_act, ACTS[n])
                        link(dve.tensor_copy(op_b[:, 0, at], G[:, j, :]))
                        dve.tensor_tensor(op_b[:, 1, at], G[:, j, :], op_b[:, 0, at].bitcast(F32), ALU.subtract).then_inc(hidden, 1)
                        if l == 0 and j % 2:
                            edge_batch(8 * fb + j // 2)
                    for t in range(NT):
                        n = JOB[f"down{l}.{fb}"] + t
                        dve.wait_ge(job_full, n + 1)
                        if fb + 1 < MLP:
                            dve.tensor_tensor(X[:, t, :], X[:, t, :], bank(n), ALU.add).then_inc(job_done, 1)
                        else:
                            row_wait(f"b2{l}")
                            link(dve.tensor_tensor(X[:, t, :], X[:, t, :], bank(n), ALU.add))
                            dve.tensor_tensor(X[:, t, :], X[:, t, :], rowv[:, row_at[f"b2{l}"] % 3, :], ALU.add).then_inc(job_done, 1)
                            if l + 1 < DEPTH and t % 4 == 3:
                                dve.wait_ge(job_done, DONES[n])
                                layer_norm(7 + 4 * l + t // 4, t // 4, G)
                        if l == 0 and t % 2:
                            edge_batch(8 * fb + 4 + t // 2)
            LN1 = 4 * DEPTH + 3

            dve.wait_ge(job_done, DONES[JOB["down1.3"] + 7])
            for h in range(2):
                raw_wait(dve, f"x{h}")
                dve.tensor_tensor(X[:, 4 * h:4 * h + 4, :].rearrange("p t n -> p (t n)"),
                                  X[:, 4 * h:4 * h + 4, :].rearrange("p t n -> p (t n)"),
                                  raw[:, raw_no[f"x{h}"] % 2, :], ALU.add).then_inc(raw_added, 1)
            dve.wait_ge(raw_added, 2)
            link(dve.tensor_copy(wg[:, 0, :, :], wg_raw[:, :, :]))
            dve.tensor_tensor(wg[:, 1, :, :], wg_raw[:, :, :], wg[:, 0, :, :].bitcast(F32), ALU.subtract).then_inc(wg_ready, 1)
            for t in range(NT):
                n = JOB["gnn"] + t
                dve.wait_ge(job_full, n + 1)
                dve.tensor_tensor(X[:, t, :], X[:, t, :], bank(n), ALU.add).then_inc(job_done, 1)
                if t % 4 == 3:
                    dve.wait_ge(job_done, DONES[n])
                    layer_norm(LN1 + t // 4, t // 4, G)
            lo_transposed("xt_T", op_a)

            n = JOB["gate"]
            bc = lambda ap: ap.unsqueeze(2).to_broadcast([P, NT, EXPERTS])
            be = lambda ap: ap.unsqueeze(1).to_broadcast([P, NT, EXPERTS])
            sc, ex1, ex2, oh1, oh2, wk = (g8[:, i, :, :] for i in (0, 2, 3, 4, 5, 1))
            m1, s1, m2, r, key = (g1[:, i, :] for i in range(5))
            dve.wait_ge(job_full, n + 1)
            dve.tensor_tensor(sc, bank(n)[:, 0:NT * EXPERTS].rearrange("p (t e) -> p t e", e=EXPERTS), be(bg[:, :]), ALU.add)\
               .then_inc(job_done, 1)
            dve.wait_ge(job_done, DONES[n])
            link(dve.tensor_reduce(m1, sc, AX_X, ALU.max))
            dve.tensor_tensor(wk, sc, bc(m1), ALU.subtract).then_inc(copied, 1)
            dve.wait_ge(achain, 1)
            link(dve.tensor_reduce(s1, wk, AX_X, ALU.add))
            link(dve.reciprocal(r, s1))
            link(dve.tensor_tensor(sc, wk, bc(r), ALU.mult))
            link(dve.tensor_reduce(m1, sc, AX_X, ALU.max))

            def first_of(dst, scores, m):
                link(dve.tensor_tensor(dst, scores, bc(m), ALU.is_equal))
                link(dve.tensor_tensor(dst, dst, be(eidx[:, :]), ALU.mult))
                link(dve.tensor_reduce(key, dst, AX_X, ALU.max))
                link(dve.tensor_tensor(dst, be(eidx[:, :]), bc(key), ALU.is_equal))

            first_of(oh1, sc, m1)
            dve.tensor_tensor(ex1, sc, bc(m1), ALU.subtract).then_inc(copied, 1)
            link(dve.scalar_tensor_tensor(out=wk, in0=oh1, scalar=-4.0, in1=sc, op0=ALU.mult, op1=ALU.add))
            link(dve.tensor_reduce(m2, wk, AX_X, ALU.max))
            first_of(oh2, wk, m2)
            dve.wait_ge(achain, 2)
            link(dve.tensor_tensor(ex2, sc, bc(m2), ALU.subtract))
            dve.tensor_scalar(ex2, ex2, 0.0, None, ALU.min).then_inc(copied, 1)
            link(dve.tensor_tensor(wk, sc, bc(m1), ALU.max))
            link(dve.tensor_scalar(wk, wk, JITTER, None, ALU.mult))
            link(dve.tensor_tensor(wk, wk, sc, ALU.add))
            link(dve.tensor_tensor(wk, wk, bc(m1), ALU.is_ge))
            link(dve.tensor_tensor(ex1, ex1, wk, ALU.mult))
            link(dve.tensor_reduce(s1, ex1, AX_X, ALU.add))
            link(dve.reciprocal(r, s1))
            link(dve.tensor_tensor(wk, sc, bc(m2), ALU.max))
            link(dve.tensor_scalar(wk, wk, JITTER, None, ALU.mult))
            link(dve.tensor_tensor(wk, wk, sc, ALU.add))
            link(dve.tensor_tensor(wk, wk, bc(m2), ALU.is_ge))
            link(dve.tensor_tensor(wk, wk, oh1, ALU.is_gt))
            dve.wait_ge(achain, 3)
            link(dve.tensor_tensor(ex2, ex2, wk, ALU.mult))
            link(dve.tensor_reduce(s1, ex2, AX_X, ALU.add))
            link(dve.reciprocal(key, s1))
            link(dve.tensor_tensor(oh1, oh1, bc(r), ALU.mult))
            link(dve.tensor_tensor(oh2, oh2, bc(key), ALU.mult))
            link(dve.tensor_tensor(comb[:, :, :], oh1, oh2, ALU.add))

            def expert(e, last, chain_loop):
                full = JOBS_PER_EXPERT * e
                for fb in range(FB):
                    base = JOB["experts"] + 24 * fb
                    if fb == 0:
                        dve.wait_ge(job_done, DONES[base - 1] + DONES_PER_EXPERT * e)
                        link(dve.tensor_copy(combe[:, :].unsqueeze(2), comb[:, :, bass.ds(e, 1)]), chain_loop)
                    for j in range(8):
                        n = base + 2 * j
                        m, c = j // 2, j % 2
                        at = slice(m * N + c * HALF, m * N + (c + 1) * HALF)
                        dve.wait_ge(job_act, ACTS[n] + ACTS_PER_EXPERT * e)
                        dve.wait_ge(job_full, n + 2 + full)
                        link(dve.tensor_tensor(G[:, j, :], G[:, j, :], bank(n + 1), ALU.mult), chain_loop)
                        link(dve.tensor_copy(op_b[:, 0, at], G[:, j, :]), chain_loop)
                        dve.tensor_tensor(op_b[:, 1, at], G[:, j, :], op_b[:, 0, at].bitcast(F32), ALU.subtract).then_inc(job_done, 1)
                    for t in range(NT):
                        n = base + 16 + t
                        dve.wait_ge(job_full, n + 1 + full)
                        ins = dve.scalar_tensor_tensor(out=X[:, t, :], in0=bank(n), scalar=combe[:, t:t + 1], in1=X[:, t, :],
                                                       op0=ALU.mult, op1=ALU.add)
                        ins.then_inc(job_done, 1)
                        if last and fb + 1 == FB and t % 4 == 3:
                            dve.wait_ge(job_done, DONES[n] + DONES_PER_EXPERT * e)
                            layer_norm(LN1 + 2 + t // 4, t // 4, G)

            per = 1 + 2 * 8 * FB
            with dve.Fori(0, EXPERTS - 1) as e:
                before = count[0]
                expert(e, False, per * e)
                assert count[0] - before == per
            count[0] += per * (EXPERTS - 2)
            expert(EXPERTS - 1, True, 0)

            lo_transposed("x3_T", op_a)
            n = JOB["deg"]
            dve.wait_ge(job_full, n + 1)
            dve.tensor_scalar(norm[:, :], bank(n)[:, 0:NT], 1.0, None, ALU.max).then_inc(job_done, 1)
            dve.wait_ge(achain, 4)
            link(dve.reciprocal(norm[:, :], norm[:, :]))
            lo_slot("wv_T", "l1_wv")
            lo_slot("wth_T", "l1_wth")
            lo_slot("kv", "kv")
            for t in range(NT):
                n = JOB["xkv"] + t
                dve.wait_ge(job_full, n + 1)
                if t == 0:
                    dve.wait_ge(job_act, ACTS[JOB["mean"]])
                link(dve.scalar_tensor_tensor(out=X[:, t, :], in0=bank(n), scalar=1.0 / (N * math.sqrt(D)), in1=X[:, t, :],
                                              op0=ALU.mult, op1=ALU.add))
                dve.tensor_tensor(X[:, t, :], X[:, t, :], mean_row[:, :], ALU.add).then_inc(job_done, 1)
            lo_slot("fc_T", "l1_fc")
            row_wait("fc_b")
            for t in range(NT):
                n = JOB["h"] + t
                dve.wait_ge(job_full, n + 1)
                dve.tensor_tensor(G[:, t, :], bank(n), rowv[:, row_at["fc_b"] % 3, :], ALU.add).then_inc(job_done, 1)
            dve.wait_ge(job_done, DONES[JOB["h"] + 7])

            def scaled_by_norm():
                for t in range(NT):
                    at = slice(t * D, (t + 1) * D)
                    link(dve.tensor_scalar(op_b[:, 0, at], G[:, t, :], norm[:, t:t + 1], None, ALU.mult))
                    ins = dve.scalar_tensor_tensor(out=op_b[:, 1, at], in0=G[:, t, :], scalar=norm[:, t:t + 1],
                                                   in1=op_b[:, 0, at].bitcast(F32), op0=ALU.mult, op1=ALU.subtract)
                ins.then_inc(xs_ready, 1)

            lo_transposed("h_T", op_a)
            for g in range(2):
                scaled_by_norm()
                for t in range(NT):
                    n = JOB[f"agg{g}"] + t
                    dve.wait_ge(job_full, n + 1)
                    dve.tensor_scalar(G[:, t, :], bank(n), norm[:, t:t + 1], 0.9, ALU.mult, ALU.mult).then_inc(job_done, 1)
                lo_transposed(f"f_T{g}", op_b)
                b = f"b_{g + 1}"
                row_wait(b)
                for t in range(NT):
                    n = JOB[f"rst{g}"] + t
                    dve.wait_ge(job_full, n + 1)
                    link(dve.tensor_tensor(tmp[:, t % 2, :], bank(n), rowv[:, row_at[b] % 3, :], ALU.add))
                    if g == 0:
                        dve.tensor_scalar(G[:, t, :], tmp[:, t % 2, :], 0.0, None, ALU.max).then_inc(job_done, 1)
                    else:
                        dve.scalar_tensor_tensor(out=X[:, t, :], in0=tmp[:, t % 2, :], scalar=0.0, in1=X[:, t, :],
                                                 op0=ALU.max, op1=ALU.add).then_inc(job_done, 1)
                    dve.wait_ge(job_done, DONES[n])
                    if g == 1 and t % 4 == 3:
                        layer_norm(LN1 + 4 + t // 4, t // 4, G)

            dve.wait_ge(ln_ready, LN1 + 5)
            link(dve.tensor_scalar(nib[:, :, :, :].rearrange("p t g j -> p t (g j)"), G[:, :, 16:80], 0.5, None, ALU.is_gt))
            link(dve.tensor_tensor(nib[:, :, :, :].rearrange("p t g j -> p (t g) j"), nib[:, :, :, :].rearrange("p t g j -> p (t g) j"),
                                   cnt16[:, 0, :].unsqueeze(1).to_broadcast([P, NT * 4, 16]), ALU.mult))
            link(dve.tensor_reduce(nibv[:, 0, :, :].rearrange("p t g -> p (t g)"), nib[:, :, :, :].rearrange("p t g j -> p (t g) j"),
                                   AX_X, ALU.max))
            dve.tensor_scalar(nibv[:, 1, :, :], nibv[:, 0, :, :], -1.0, 16.0, ALU.mult, ALU.add)
            link(dve.tensor_scalar(nibv[:, 2, :, :], nibv[:, 0, :, :], 0.0, None, ALU.is_gt))
            for pos in range(2):
                dve.tensor_tensor(u[:, pos, :, 0], nibv[:, 1, :, pos], nibv[:, 2, :, pos], ALU.mult)
                dve.tensor_tensor(u[:, pos, :, 1], nibv[:, 1, :, 2 + pos], nibv[:, 2, :, 2 + pos], ALU.mult)
                ins = dve.tensor_copy(u[:, pos, :, 2:4], G[:, :, 105:107])
            ins.then_inc(u_ready, 1)
            for i in range(3):
                ins = dve.tensor_scalar(masks[:, i, :], G[:, :, i], 0.5, None, ALU.is_gt)
            link(ins)
            link(dve.tensor_tensor(masks[:, 3, :], masks[:, 0, :], masks[:, 1, :], ALU.mult))
            link(dve.tensor_tensor(masks[:, 4, :], masks[:, 0, :], masks[:, 3, :], ALU.subtract))
            link(dve.tensor_tensor(masks[:, 4, :], masks[:, 4, :], masks[:, 2, :], ALU.mult))
            link(dve.tensor_tensor(masks[:, 5, :], masks[:, 3, :], masks[:, 4, :], ALU.add))
            for j in range(4):
                n = JOB["u_T"] + j
                dve.wait_ge(job_full, n + 1)
                dve.tensor_copy(u_T[:, j // 2, (j % 2) * HALF:(j % 2 + 1) * HALF], bank(n)[0:4, :]).then_inc(job_done, 1)
            for p in range(2):
                n = JOB["w1_T"] + p
                dve.wait_ge(job_full, n + 1)
                dve.tensor_copy(w1_T[:, p, 0, :], bank(n)[:, 0:GE])
                dve.tensor_copy(w1_T[0:GE_LO, p, 1, :], bank(n)[0:GE_LO, GE:2 * GE]).then_inc(job_done, 1)
            for i in range(8):
                p, pos, c = i // 4, i // 2 % 2, i % 2
                base = JOB["alu"] + 5 * i
                n = base + 4
                dve.wait_ge(job_full, n + 1)
                dve.tensor_tensor(yo[:, p, pos, 4 * c:4 * c + 4, :], bank(n)[:, 0:8].rearrange("p (t o) -> p t o", o=2),
                                  b_out[:, p, :].unsqueeze(1).to_broadcast([P, 4, 2]), ALU.add).then_inc(job_done, 1)
            dve.wait_ge(job_done, DONES[JOB["alu"] + 39])
            yf = yo[:, :, :, :, :].rearrange("p a b t o -> p (a b t o)")
            link(dve.tensor_scalar(yf, yf, 0.0, 15.0, ALU.max, ALU.min))
            link(dve.tensor_scalar(yf, yf, ROUNDER, None, ALU.add))
            link(dve.tensor_scalar(yf, yf, -ROUNDER, None, ALU.add))
            for p in range(2):
                y3 = yo[:, p, :, :, :].rearrange("p b t o -> p b (t o)")
                mk = masks[:, 3 + p, :].unsqueeze(2).to_broadcast([P, NT, 2])
                for pos in range(2):
                    ins = dve.tensor_tensor(yo[:, p, pos, :, :], yo[:, p, pos, :, :], mk, ALU.mult)
            link(ins)
            link(dve.tensor_tensor(yo[:, 0, :, :, :].rearrange("p b t o -> p (b t o)"), yo[:, 0, :, :, :].rearrange("p b t o -> p (b t o)"),
                                   yo[:, 1, :, :, :].rearrange("p b t o -> p (b t o)"), ALU.add))
            for pos in range(2):
                ins = dve.tensor_tensor(onehot[:, pos, :, :], cnt16[:, 1, :].unsqueeze(1).to_broadcast([P, NT, 16]),
                                        yo[:, 0, pos, :, 0].unsqueeze(2).to_broadcast([P, NT, 16]), ALU.is_equal)
            link(ins)
            for pos in range(2):
                ins = dve.tensor_tensor(onehot[:, pos, :, :], onehot[:, pos, :, :],
                                        masks[:, 5, :].unsqueeze(2).to_broadcast([P, NT, 16]), ALU.mult)
            link(ins)
            link(dve.tensor_scalar(masks[:, 0, :], yo[:, 0, 1, :, 1], 0.5, None, ALU.is_gt))
            for pos in range(2):
                at = slice(OUT_LO + 16 * pos, OUT_LO + 16 * pos + 16)
                dve.scalar_tensor_tensor(out=G[:, :, at], in0=onehot[:, pos, :, :], scalar=2.0, in1=G[:, :, at],
                                         op0=ALU.mult, op1=ALU.add)
            link(dve.tensor_tensor(G[:, :, CARRY], G[:, :, CARRY], masks[:, 0, :], ALU.add))
            dve.tensor_tensor(X[:, :, :].rearrange("p t n -> p (t n)"), X[:, :, :].rearrange("p t n -> p (t n)"),
                              G[:, :, :].rearrange("p t n -> p (t n)"), ALU.add).then_inc(out_ready, 1)

        @block.gpsimd
        def _(pool):
            count = [0]

            def link(ins):
                count[0] += 1
                ins.then_inc(pchain, 1)
                pool.wait_ge(pchain, count[0])

            def lo(name):
                r = raw_no[name]
                pool.wait_ge(hi_done, split_no[name] + 1)
                if name.startswith("hg"):
                    h = int(name[2])
                    hi_at, lo_at = (op_a[:, i, h * BLK:(h + 1) * BLK] for i in range(2))
                else:
                    s = slot_of[name] % SLOTS
                    hi_at, lo_at = W[:, s, 0, :], W[:, s, 1, :]
                pool.tensor_tensor(lo_at, raw[:, r % 2, :], hi_at.bitcast(F32), ALU.subtract).then_inc(lo_done, 1)

            link(pool.memset(ident[:, :], 0.0))
            pool.affine_select(out=ident[:, :], in_=ident[:, :], compare_op=ALU.not_equal, fill=1.0, base=0,
                               pattern=[[-1, P]], channel_multiplier=1)
            pool.memset(ones[:, :], 1.0)
            pool.memset(eps_ones[:, :], KERNEL_EPS)
            pool.memset(lneps[:, :], LN_EPS)
            pool.memset(vsum[:, :, DH:VW], KERNEL_EPS * N)
            link(pool.memset(head_sel[:, :], 0.0))
            pool.memset(head_sel[0:DH, 0:1], 0.5 * NORMALIZER ** 2)
            link(pool.memset(head_sel[DH:P, 1:2], 0.5 * NORMALIZER ** 2))
            pool.iota(trash[:, :], [[0, 1]], base=TABLE, channel_multiplier=1, allow_small_or_imprecise_dtypes=True)
            pool.iota(eidx[:, :], [[-1, EXPERTS]], base=EXPERTS, channel_multiplier=0, allow_small_or_imprecise_dtypes=True)
            link(pool.memset(proj[:, :, :], 0.0))
            link(pool.memset(zero[:, :], 0.0))
            pool.affine_select(out=lower[:, :], in_=ones[:, :], compare_op=ALU.is_gt, fill=0.0, base=0,
                               pattern=[[-1, P]], channel_multiplier=1).then_inc(consts, 1)
            for tb in (table_w, table_c):
                for h in range(2):
                    pool.dma_start(tb[h * (TABLE // 2):(h + 1) * (TABLE // 2), :].rearrange("(p n) o -> p (n o)", p=P), zero[:, :])\
                        .then_inc(zeroed, 16)
            for tb in (table_w, table_c):
                pool.dma_start(tb[TABLE:TABLE + P, :], zero[:, 0:1]).then_inc(trash_zeroed, 16)
            pool.wait_ge(zeroed, 64)
            pool.wait_ge(trash_zeroed, 32)
            for i, name in enumerate(("src", "dst")):
                pool.dma_start(edge_int[:, i, :], a[name].rearrange("(c p) -> c p", p=P)).then_inc(edge_loaded, 16)
            pool.dma_start(edge_f[:, 4, :], a["edge_weight"].rearrange("(c p) -> c p", p=P)).then_inc(edge_loaded, 16)
            pool.wait_ge(keys_ready, 1)
            pool.dma_start(key_dram.rearrange("(c p) -> c p", p=P), edge_f[:, 2, :]).then_inc(key_stored, 16)

            def projection(l):
                if l:
                    pool.wait_ge(job_full, JOB[f"proj{l - 1}"] + 1)
                for i in range(2):
                    for h in range(2):
                        pool.dma_start(proj_nat[:, i, h, :], a["L0_mix_proj"][l][i * P:(i + 1) * P, :]).then_inc(proj_loaded, 16)

            def edge_rows(b):
                if b == 0:
                    pool.wait_ge(key_stored, 16)
                    pool.wait_ge(job_full, JOB["o_T0"])
                else:
                    pool.wait_ge(edge_row_free, b)
                    pool.wait_ge(edge_ready, b)
                at = slice(b * EB * P, (b + 1) * EB * P)
                pool.dma_start(key_row[:, :, :].rearrange("p c j -> p (c j)"), key_dram[at].partition_broadcast(P)).then_inc(edge_row, 16)
                pool.dma_start(w_row[:, :, :].rearrange("p c j -> p (c j)"), a["edge_weight"][at].partition_broadcast(P))\
                    .then_inc(edge_row, 16)

            scattered = [0]

            def scatter(n):
                for _ in range(n):
                    c = scattered[0]
                    if c == EC:
                        return
                    if c % EB == 0:
                        pool.wait_ge(edge_ready, c // EB + 1)
                    for i, tb in enumerate((table_w, table_c)):
                        if c:
                            pool.wait_ge(added[i], 16 * c)
                        pool.indirect_dma_start(out=tb, out_offset=bass.IndirectOffsetOnAxis(ap=edge_ix[:, i, c:c + 1].bitcast(U32), axis=0),
                                                in_=edge_add[:, i, c:c + 1], in_offset=None, compute_op=ALU.add).then_inc(added[i], 16)
                    scattered[0] += 1

            projection(0)
            for l in range(DEPTH):
                for name in ("wq", "wk", "wv", "wo"):
                    lo(f"{name}{l}")
                    if l:
                        scatter(5)
                lo(f"up{l}.0")
                for hp in range(HEADS // 2):
                    pool.wait_ge(kmax_ready, 4 * l + hp + 1)
                    pool.partition_all_reduce(kmaxp[:, 1, :], kmaxp[:, 0, :], P, bass.bass_isa.ReduceOp.max).then_inc(kmax_all, 1)
                    if l:
                        scatter(8)
                lo(f"down{l}.0")
                if l + 1 < DEPTH:
                    projection(l + 1)
                for fb in range(MLP):
                    nb = 8 * fb
                    if l == 0:
                        for b in range(nb, nb + 4):
                            edge_rows(b)
                    else:
                        scatter(5)
                    if fb + 1 < MLP:
                        lo(f"up{l}.{fb + 1}")
                    if l == 0:
                        for b in range(nb + 4, nb + 8):
                            edge_rows(b)
                        scatter(6)
                    else:
                        scatter(5)
                    if fb + 1 < MLP:
                        lo(f"down{l}.{fb + 1}")
            scatter(EC)
            for h in range(2):
                lo(f"hg{h}")
            for q in range(4):
                lo(f"adj{q}")
            lo("e0.w1.0")
            lo("e0.w3.0")

            def expert_lo(k, e, nxt=0):
                s = (slot_of["e0.w1.0"] + k) % SLOTS
                r = (raw_no["e0.w1.0"] + k) % 2
                pool.wait_ge(hi_done, split_no["e0.w1.0"] + k + 1 + 3 * FB * nxt + 3 * FB * e)
                pool.tensor_tensor(W[:, s, 1, :], raw[:, r, :], W[:, s, 0, :].bitcast(F32), ALU.subtract).then_inc(lo_done, 1)

            with pool.Fori(0, EXPERTS - 1) as e:
                for k in range(2, 3 * FB):
                    expert_lo(k, e)
                for k in range(2):
                    expert_lo(k, e, 1)
            for k in range(2, 3 * FB):
                expert_lo(k, EXPERTS - 1)

            def gcn_scale(g, which):
                name = f"gw{which}.{g}"
                beta = float(np.log(1.0 / (g + 1) + 1.0))
                by = 0.1 if which == 2 else 1.0
                r = raw_no[name]
                rb = raw[:, r % 2, :]
                raw_wait(pool, name)
                link(pool.tensor_scalar(rb, rb, beta * by, 1.0, ALU.mult, ALU.mult))
                link(pool.tensor_scalar(lower[:, :], ident[:, :], (1.0 - beta) * by, 1.0, ALU.mult, ALU.mult))
                for k in range(NK):
                    at = slice(k * D + k * P, k * D + (k + 1) * P)
                    ins = pool.tensor_tensor(raw[:, r % 2, at], raw[:, r % 2, at], lower[:, :], ALU.add)
                ins.then_inc(scaled, 1)

            pool.wait_ge(job_done, DONES[JOB["experts"] + 1])
            for p, (w, b) in enumerate((("L1_ffn_Wa", "L1_ffn_ba"), ("L1_ffn_Ws", "L1_ffn_bs"))):
                with nc.allow_non_contiguous_dma(reason="a few hundred numbers"):
                    for i, col in enumerate((0, 35)):
                        pool.dma_start(w0_T[2 * i:2 * i + 2, p, :], a[w][0, :, col:col + 2].rearrange("o c -> c o")).then_inc(nibble_loaded, 16)
                    pool.dma_start(wn_a[:, p, :], a[w][1, 0:P, :]).then_inc(nibble_loaded, 16)
                    pool.dma_start(wn_b[:, p, :], a[w][1, P:GE, :]).then_inc(nibble_loaded, 16)
                    for k, (i0, i1) in enumerate(((0, P), (P, GE))):
                        pool.dma_start(w2_T[0:i1 - i0, p, k, :], a[w][2, RESULT:RESULT + 2, i0:i1].rearrange("o i -> i o")).then_inc(nibble_loaded, 16)
                        for layer in range(2):
                            pool.dma_start(b_hid[0:i1 - i0, p, layer, k:k + 1], a[b][layer, i0:i1].rearrange("(i o) -> i o", o=1)).then_inc(nibble_loaded, 16)
                    pool.dma_start(b_out[:, p, :], a[b][2, RESULT:RESULT + 2].partition_broadcast(P)).then_inc(nibble_loaded, 16)
            pool.iota(cnt16[:, 0, :], [[-1, 16]], base=16, channel_multiplier=0, allow_small_or_imprecise_dtypes=True)
            link(pool.iota(cnt16[:, 1, :], [[1, 16]], base=0, channel_multiplier=0, allow_small_or_imprecise_dtypes=True))
            for g in range(2):
                for q in range(4):
                    lo(f"cnt{g}.{q}")
                gcn_scale(g, 1)
                lo(f"gw1.{g}")
                gcn_scale(g, 2)
                lo(f"gw2.{g}")


PARAMS_MIX = 7 * DEPTH + 2
PARAMS_NIBBLE = 2 * 11


def kernel(**inputs):
    import numpy as _np
    import concourse.bacc as _bacc
    from concourse import mybir as _mybir
    from concourse.bass_utils import run_bass_kernel_spmd as _run

    nc = _bacc.Bacc("TRN2", target_bir_lowering=False, num_devices=1)
    arrays, aps = {}, {}
    for name in inputs:
        v = _np.ascontiguousarray(inputs[name])
        arrays[f"in_{name}_dram"] = v
        aps[name] = nc.dram_tensor(f"in_{name}_dram", v.shape, _mybir.dt.from_np(v.dtype), kind="ExternalInput").ap()
    out = nc.dram_tensor("out_0_dram", (N, D), F32, kind="ExternalOutput").ap()
    gps_network(nc, aps, out)
    r = _run(nc, [arrays], core_ids=[0])
    return r.results[0]["out_0_dram"]
```
